# Optimizing a Trainium2 kernel written in Bass

```python
import numpy as np
import jax
import jax.numpy as jnp

def _softmax(x, axis=-1):
    return jax.nn.softmax(x, axis=axis)

def _gelu(x):
    return jax.nn.gelu(x, approximate=True)

def _silu(x):
    return jax.nn.silu(x)

def _sigmoid(x):
    return jax.nn.sigmoid(x)

def _layernorm(x, axis=-1, eps=1e-05):
    m = jnp.mean(x, axis=axis, keepdims=True)
    v = jnp.var(x, axis=axis, keepdims=True)
    return (x - m) / jnp.sqrt(v + eps)

def _scatter_add(tgt, idx, src, axis=0):
    return tgt.at[idx].add(src)

def _segment_sum(src, seg, n):
    return jax.ops.segment_sum(src, seg, n)
kernel_name = 'mk_macaron_d1_jaxref_r4_18c11b'

def setup_inputs(seed: int=0):
    np.random.seed(seed)
    _w = jnp.asarray

    def _L0_attn_setup():
        import jax, jax.numpy as jnp
        import numpy as np
        import math
        E, N, K, R = (256, 16, 4, 64)
        B, L = (2, 512)
        key = jax.random.key(seed)
        ks = jax.random.split(key, 8)
        gn = lambda k, sh, sc: jax.random.normal(k, sh, dtype=jnp.float32) * sc
        W_z = gn(ks[0], (E, E), E ** (-0.5))
        W_params = gn(ks[1], (R + 2 * N, E), E ** (-0.5))
        conv_w = gn(ks[2], (E, 1, K), 0.5)
        dt_std = R ** (-0.5) * 0.1
        W_dt = jax.random.uniform(ks[3], (E, R), jnp.float32, -dt_std, dt_std)
        b_dt = jnp.full((E,), math.log(math.expm1(0.001)), dtype=jnp.float32)
        A_log = jnp.tile(jnp.log(jnp.arange(1, N + 1, dtype=jnp.float32))[None, :], (E, 1))
        D = jnp.ones((E,), dtype=jnp.float32)
        W_out = gn(ks[4], (E, E), E ** (-0.5))
        x = jax.random.normal(ks[5], (B, L, E), dtype=jnp.float32)
        return dict(x=x, W_z=W_z, W_params=W_params, conv_w=conv_w, W_dt=W_dt, b_dt=b_dt, A_log=A_log, D=D, W_out=W_out)
    _L0_attn_in = _L0_attn_setup()

    def _L0_ffn_setup():
        import jax, jax.numpy as jnp
        import numpy as np
        DIM = 256
        HIDDEN = 768
        SCALE = 1.0 / 127.0

        def _dequant(w_int, dtype):
            return w_int.astype(dtype) * jnp.asarray(SCALE, dtype)
        key = jax.random.key(seed)
        k_x, k_g, k_u, k_d = jax.random.split(key, 4)
        x = jax.random.normal(k_x, (4, 512, DIM), dtype=jnp.float32)
        w_gate = jax.random.randint(k_g, (HIDDEN, DIM), -127, 128, dtype=jnp.int32)
        w_up = jax.random.randint(k_u, (HIDDEN, DIM), -127, 128, dtype=jnp.int32)
        w_down = jax.random.randint(k_d, (DIM, HIDDEN), -127, 128, dtype=jnp.int32)
        return {'x': x, 'w_gate': w_gate, 'w_up': w_up, 'w_down': w_down}
    _L0_ffn_in = _L0_ffn_setup()
    _d = {'L0_attn_x': _L0_attn_in['x'], 'L0_attn_W_z': _L0_attn_in['W_z'], 'L0_attn_W_params': _L0_attn_in['W_params'], 'L0_attn_conv_w': _L0_attn_in['conv_w'], 'L0_attn_W_dt': _L0_attn_in['W_dt'], 'L0_attn_b_dt': _L0_attn_in['b_dt'], 'L0_attn_A_log': _L0_attn_in['A_log'], 'L0_attn_D': _L0_attn_in['D'], 'L0_attn_W_out': _L0_attn_in['W_out'], 'L0_ffn_w_gate': _L0_ffn_in['w_gate'], 'L0_ffn_w_up': _L0_ffn_in['w_up'], 'L0_ffn_w_down': _L0_ffn_in['w_down']}
    _x0 = _d['L0_attn_x']
    _d['L0_attn_x'] = jax.random.normal(jax.random.fold_in(jax.random.key(seed), 1), (16, 1024, 256), dtype=_x0.dtype)
    del _x0
    return _d

def reference(L0_attn_x, L0_attn_W_z, L0_attn_W_params, L0_attn_conv_w, L0_attn_W_dt, L0_attn_b_dt, L0_attn_A_log, L0_attn_D, L0_attn_W_out, L0_ffn_w_gate, L0_ffn_w_up, L0_ffn_w_down):

    def _L0_attn_ref(x, W_z, W_params, conv_w, W_dt, b_dt, A_log, D, W_out):
        import jax, jax.numpy as jnp
        import numpy as np
        import math
        E, N, K, R = (256, 16, 4, 64)
        B, L = (2, 512)
        b, l, e = x.shape
        n = A_log.shape[1]
        r = W_dt.shape[1]
        k = conv_w.shape[-1]
        z = x @ W_z.T
        params = x @ W_params.T
        dt_unproj = params[..., :r]
        C_proj = params[..., r + n:]
        dt = jax.nn.softplus(dt_unproj @ W_dt.T + b_dt)
        xc = jax.lax.conv_general_dilated(x.transpose(0, 2, 1), conv_w, (1,), [(k - 1, 0)], dimension_numbers=('NCH', 'OIH', 'NCH'), feature_group_count=e)
        u = jax.nn.silu(xc.transpose(0, 2, 1))
        A = -jnp.exp(A_log)
        A_tilde = jnp.exp(dt[..., None] * A[None, None])
        B_tilde = jnp.where(jnp.abs(A)[None, None] < 1e-05, dt[..., None], (A_tilde - 1.0) / (A[None, None] + 1e-10))
        h0 = B_tilde[:, 0] * u[:, 0, :, None]

        def step(h, inp):
            a, bt, uu = inp
            h_new = a * h + bt * uu[..., None]
            return (h_new, h_new)
        xs = (A_tilde[:, :-1].transpose(1, 0, 2, 3), B_tilde[:, :-1].transpose(1, 0, 2, 3), u[:, :-1].transpose(1, 0, 2))
        _, hs = jax.lax.scan(step, h0, xs)
        h = jnp.concatenate([h0[None], hs], axis=0).transpose(1, 0, 2, 3)
        y = jnp.einsum('bln,blen->ble', C_proj, h)
        y_ssm = y + u * D
        y_gated = y_ssm * jax.nn.silu(z)
        return y_gated @ W_out.T

    def _L0_ffn_ref(x, w_gate, w_up, w_down):
        import jax, jax.numpy as jnp
        import numpy as np
        DIM = 256
        HIDDEN = 768
        SCALE = 1.0 / 127.0

        def _dequant(w_int, dtype):
            return w_int.astype(dtype) * jnp.asarray(SCALE, dtype)
        wg = _dequant(w_gate, x.dtype)
        wu = _dequant(w_up, x.dtype)
        wd = _dequant(w_down, x.dtype)
        gate = jnp.einsum('bsd,hd->bsh', x, wg)
        up = jnp.einsum('bsd,hd->bsh', x, wu)
        h = jax.nn.silu(gate) * up
        return jnp.einsum('bsh,dh->bsd', h, wd)
    x = L0_attn_x
    x = x + 0.5 * _L0_ffn_ref(_layernorm(x, axis=-1), L0_ffn_w_gate, L0_ffn_w_up, L0_ffn_w_down)
    x = x + _L0_attn_ref(_layernorm(x, axis=-1), L0_attn_W_z, L0_attn_W_params, L0_attn_conv_w, L0_attn_W_dt, L0_attn_b_dt, L0_attn_A_log, L0_attn_D, L0_attn_W_out)
    x = x + 0.5 * _L0_ffn_ref(_layernorm(x, axis=-1), L0_ffn_w_gate, L0_ffn_w_up, L0_ffn_w_down)
    return x

_drawn_inputs = setup_inputs


def setup_inputs(seed=0):
    import zlib

    import numpy as np

    out = dict(_drawn_inputs(seed))
    spreads = {'L0_attn_b_dt': (-6.907255172729492, 0.6), 'L0_attn_D': (1.0, 0.6)}
    factors = {'L0_attn_W_z': 8.0,
     'L0_attn_W_params': 8.0,
     'L0_attn_conv_w': 8.0,
     'L0_attn_W_dt': 8.0,
     'L0_attn_A_log': 8.0,
     'L0_attn_W_out': 8.0}
    for name, (base, spread) in spreads.items():
        noise = np.random.default_rng([zlib.crc32(name.encode()), seed]).standard_normal(out[name].shape)
        drawn = base * np.exp(spread * noise) if base else spread * noise
        out[name] = jnp.asarray(drawn.astype(out[name].dtype))
    for name, factor in factors.items():
        out[name] = (out[name] * factor).astype(out[name].dtype)
    return out
```

```python
from contextlib import ExitStack

import numpy as np

import concourse.bass as bass
from concourse import mybir

ALU = mybir.AluOpType
ACT = mybir.ActivationFunctionType
AX_X = mybir.AxisListType.X
F32 = mybir.dt.float32
F32R = mybir.dt.float32r
F16 = mybir.dt.float16
I32 = mybir.dt.int32

P = 128
B, L, E = 16, 1024, 256
HID = 768
N, KW, R = 16, 4, 64
EH = E // P
CH = 512
NC = L // CH
TJ = CH // P
HM = HID // P
TANHS = 4
BANKS = 6
EPS = 1e-5
A_MIN = 1e-5
XS = 1024.0
Q = 127.0
GATE_HALF = 0.5 / (XS * Q)
H_SCALE = 0.25 / (XS * Q) ** 2
OUT_SCALE = 1.0 / Q
C_ROW, CD_ROW = 64, 96
PROWS = CD_ROW + N
LOOP_FROM, LOOP_TO = 2, 14


def steps(b):
    ssm, ffn1, ffn2, ln1 = 0 <= b < B, 0 <= b + 1 < B, 0 <= b - 1 < B, 1 <= b + 2 < B
    at = {q: [] for q in range(2 * N)}
    tail = []

    def put(q, *ev):
        (at[q] if q < 2 * N else tail).append(ev)

    def ffn(f, bt, q0):
        order = [(c, m) for c in range(NC) for m in range(HM)]
        for i, (c, m) in enumerate(order):
            q = q0 + i + c
            put(q, "gu", f, bt, c, m)
            put(q + 1, "sh", f, bt, c, m)
            put(q + 2, "hl", f, bt, c, m)
        for c in range(NC):
            q = q0 + (c + 1) * (HM + 1) + 1
            put(q, "dn", f, bt, c, 0)
            put(q, "dn", f, bt, c, 1)
            put(q + 1, "rs", f, bt, c, 0)
            put(q + 1, "rs", f, bt, c, 1)

    out = []
    if b == -1:
        for c in range(NC):
            out += [("ld", 0, c), ("ln", 1, 0, c), ("T", 1, 0, c), ("Tl", 1, 0, c)]
    if ffn2:
        put(1, "gate", b - 1)
        for jp in range(2 * NC):
            put(2, "op", b - 1, jp)
            put(3, "ra", b - 1, jp)
    if ssm:
        for c in range(NC):
            for h in range(EH):
                put(3 + c, "z", b, h, c)
                put(4 + c, "zs", b, h, c)
    if ffn2:
        put(5, "ln", 3, b - 1, 0)
        put(8, "T", 3, b - 1, 0)
        put(9, "Tl", 3, b - 1, 0)
        put(13, "ln", 3, b - 1, 1)
        put(15, "T", 3, b - 1, 1)
        put(16, "Tl", 3, b - 1, 1)
    if ffn1:
        ffn(1, b + 1, 0)
        put(10, "ln", 2, b + 1, 0)
        put(12, "T", 2, b + 1, 0)
        put(17, "ln", 2, b + 1, 1)
        put(18, "T", 2, b + 1, 1)
        put(19, "pm", b + 1, 0)
        put(19, "pm", b + 1, 1)
        put(20, "pl", b + 1)
        for c in range(NC):
            for h in range(EH):
                put(20 + c, "cv", b + 1, h, c)
                put(21 + c, "us", b + 1, h, c)
        put(22, "u0", b + 1)
        for h in range(EH):
            for c in range(NC):
                put(22 + 2 * h, "dt", b + 1, h, c)
            for c in range(NC):
                put(22 + 2 * h, "ln1p", b + 1, h, c)
            for c in range(NC):
                put(23 + 2 * h, "dr", b + 1, h, c)
            for c in range(NC):
                put(23 + 2 * h, "dts", b + 1, h, c)
            for c in range(NC):
                put(24 + 2 * h, "dtf", b + 1, h, c)
        put(27, "dt0", b + 1)
        for h in range(EH):
            for c in range(NC):
                put(27 + h, "rm", b + 1, h, c)
                put(28 + h, "ai", b + 1, h, c)
    if ln1:
        for c in range(NC):
            put(17, "ld", b + 2, c)
            put(21 + 6 * c, "ln", 1, b + 2, c)
            put(23 + 6 * c, "T", 1, b + 2, c)
            put(24 + 6 * c, "Tl", 1, b + 2, c)
    if ffn2:
        ffn(2, b - 1, 14)
    for q in range(2 * N):
        if ssm:
            out.append(("scan", b, q // EH, q % EH))
        out += at[q]
        if ssm:
            if q:
                out.append(("cm", b, (q - 1) // EH, (q - 1) % EH))
            if q % EH == 0:
                out.append(("bc", b, q // EH))
    if ssm:
        out.append(("cm", b, N - 1, EH - 1))
    out += tail
    if ffn1:
        for h in range(EH):
            out.append(("d", b + 1, h))
    if ffn2:
        for c in range(NC):
            out.append(("st", b - 1, c))
    return out


class Counts:

    def __init__(self):
        self.at, self.bank, self.prev, self.total, self.was = {}, {}, {}, {}, {}
        last = {}
        self.slope = {}
        count, jobs, order = {}, 0, {}
        for b in range(-1, B + 1):
            for ev in steps(b):
                kind = ev[0]
                if kind == "T" and ev[1] != 2:
                    self.was[ev] = last.get(("gu", ev[3]))
                elif kind == "hl":
                    self.was[ev] = last.get("dn")
                elif kind == "ln":
                    self.was[ev] = last.get("T")
                if kind in ("ln", "T"):
                    assert last.get("row", "T") != kind, "rows are normalised and transposed in turns"
                    last["row"] = kind
                if kind == "gu":
                    last["gu", ev[3]] = ev + ("up",)
                elif kind == "dn":
                    last["dn"] = ev
                elif kind == "T":
                    last["T"] = ev + (EH - 1,)
                for job in self.jobs(ev):
                    k = jobs % BANKS
                    self.bank[job] = k
                    self.at["ready", job] = self.at["free", job] = (k, jobs // BANKS + 1)
                    jobs += 1
                for sem, n in self.increments(ev):
                    for i in range(n):
                        count[sem] = count.get(sem, 0) + 1
                    self.at[sem, ev] = (sem, count[sem])
                    before = order.setdefault(sem, [])
                    self.prev[sem, ev] = list(before[-TANHS:])
                    before.append(ev)
            self.total[b] = dict(count, jobs=jobs)
        one, two = self.total[LOOP_FROM - 1], self.total[LOOP_FROM + 1]
        self.slope = {s: two[s] - one[s] for s in two if s != "jobs"}
        assert (two["jobs"] - one["jobs"]) % BANKS == 0
        self.bank_slope = (two["jobs"] - one["jobs"]) // BANKS

    @staticmethod
    def jobs(ev):
        kind = ev[0]
        if kind == "gu":
            return [ev + ("gate",), ev + ("up",)]
        if kind == "T":
            return [ev + (h,) for h in range(EH)]
        return [ev] if kind in ("dn", "op", "z", "pm", "cv", "dt", "rm") else []

    @staticmethod
    def increments(ev):
        kind = ev[0]
        if kind in ("gu", "z", "cv"):
            return [("tanh", 1)]
        if kind == "hl":
            return [("hi", 1), ("lo", 1)]
        if kind == "ln":
            return [("stats", 1), ("meanvar", 1), ("rstd", 5), ("normed", 1)]
        if kind == "T":
            return [("xhi", EH)] if ev[1] != 2 else []
        if kind == "scan":
            return [("decay", 1), ("scanned", 1)]
        if kind == "cm":
            return [("weighted", 1), ("summed", 1)]
        one = {"bc": "c_spread", "gate": "gated", "pm": "c_high", "u0": "u_first", "dt0": "dt_first", "ai": "acc_begun",
               "d": "du", "dt": "sp_exp", "ln1p": "sp_ln", "dts": "sp_sum", "dtf": "sp_added"}
        if kind in one:
            return [(one[kind], {"gate": EH, "dt": 2, "dts": 3}.get(kind, 1))]
        if kind in ("ld", "st"):
            return [(f"{kind}{ev[2]}", 16)]
        return []


def macaron_kernel(nc, x, W_z, W_params, conv_w, W_dt, b_dt, A_log, D, W_out, w_gate, w_up, w_down, out):
    K = Counts()

    with ExitStack() as ctx:
        def sb(name, shape, dt=F32):
            return ctx.enter_context(nc.sbuf_tensor(name, shape, dt))

        def sem(name):
            return ctx.enter_context(nc.semaphore(name))

        x_in = sb("x_in", [P, NC * TJ, E])
        x_mid = [sb(f"x_mid{i}", [P, NC * TJ, E]) for i in range(2)]
        x_fin = sb("x_fin", [P, NC * TJ, E])
        normed = sb("normed", [P, TJ, E])
        stats = sb("stats", [P, 2, TJ, 6])
        meanvar = sb("meanvar", [P, 2, TJ, 2])
        rstd = sb("rstd", [P, 2, TJ])
        shift = sb("shift", [P, 2, TJ])
        xt_hi = [sb(f"xt_hi{i}", [P, EH, CH], F16) for i in range(2)]
        xt_lo = [sb(f"xt_lo{i}", [P, EH, CH], F16) for i in range(2)]
        xt = sb("xt", [P, EH, KW - 1 + L])
        tanh = sb("tanh", [P, TANHS, CH])
        hid = sb("hid", [P, 2, CH])
        hid_hi = sb("hid_hi", [P, HM, CH], F16)
        hid_lo = sb("hid_lo", [P, HM, CH], F16)
        zs = sb("zs", [P, EH, L])
        u = [sb(f"u{i}", [P, EH, 2 + L]) for i in range(2)]
        du = sb("du", [P, EH, L])
        dt = [sb(f"dt{i}", [P, EH, 1 + L]) for i in range(2)]
        params = sb("params", [P, L])
        c_parts = [sb(f"c_parts{i}", [P, L], F32R) for i in range(2)]
        ring = sb("ring", [P, 6, L])
        decay, g, cg = ring[:, 0:2, :], ring[:, 2:4, :], ring[:, 4:6, :]
        acc = [sb(f"acc{i}", [P, EH, L]) for i in range(2)]
        sp_l = sb("sp_l", [P, 2, CH])
        sp_r = sb("sp_r", [P, 2, CH])
        sp_v = sb("sp_v", [P, CH])
        wg_t = sb("wg_t", [P, EH, HID], F16)
        wu_t = sb("wu_t", [P, EH, HID], F16)
        wd_t = sb("wd_t", [P, HM, E], F16)
        wz_t = sb("wz_t", [P, EH, E])
        wp_t = sb("wp_t", [P, EH, PROWS])
        wdt_t = sb("wdt_t", [R + 1, E])
        wo_t = sb("wo_t", [P, EH, E])
        taps = sb("taps", [P, EH, KW])
        tap_diag = sb("tap_diag", [P, EH, KW, P])
        ident = sb("ident", [P, P])
        pick = sb("pick", [P, N], F32R)
        ones = sb("ones", [P, 1])
        minus_half, eps = sb("minus_half", [P, TJ]), sb("eps", [P, TJ])
        a_coef = sb("a_coef", [P, EH, N])
        inv_a = sb("inv_a", [P, EH, N])
        inv_a_t = sb("inv_a_t", [P, E])
        tiny = sb("tiny", [P, EH, N])
        kept = sb("kept", [P, EH, N])
        d_skip = sb("d_skip", [P, EH])
        flag = sb("flag", [1, 1], I32)
        flag_f = sb("flag_f", [1, 1])

        inv_a_u = hid[:, 0, 0:EH * PROWS].rearrange("p (h n) -> p h n", h=EH)
        flat = ring[:].rearrange("p s n -> p (s n)")
        st_g = flat[:, 0:HM * E]
        st_u = flat[:, HM * E:2 * HM * E]
        st_d = flat[:, 2 * HM * E:3 * HM * E]
        o = 3 * HM * E
        st_z, st_o = flat[:, o:o + EH * E], flat[:, o + EH * E:o + 2 * EH * E]
        o += 2 * EH * E
        st_p, st_dt = flat[:, o:o + E], flat[:, o + E:o + E + EH * R]

        work = [ctx.enter_context(nc.psum_tensor(f"work{i}", [P, CH], F32)) for i in range(BANKS)]
        c_bank = ctx.enter_context(nc.psum_tensor("c_bank", [P, L], F32))

        ready = [sem(f"bank_ready{i}") for i in range(BANKS)]
        free = [sem(f"bank_free{i}") for i in range(BANKS)]
        S = {s: sem(s) for s in K.slope}
        w_landed, w_set, w_turned, w_kept = sem("w_landed"), sem("w_set"), sem("w_turned"), sem("w_kept")
        s_ident, s_exp, s_set, s_flag, s_fix = sem("s_ident"), sem("s_exp"), sem("s_set"), sem("s_flag"), sem("s_fix")

        def wait(eng, what, step, turn, less=0, apart=False):
            if (what, step) not in K.at:
                return
            s, n = K.at[what, step]
            n -= less
            if what in ("ready", "free"):
                s, slope = (ready if what == "ready" else free)[s], K.bank_slope
            else:
                s, slope = S[s], K.slope[s]
            if turn is not None:
                n = eng.to_reg(turn * slope + n) if apart else turn * slope + n
                if apart:
                    eng.wait_ge(s_set, 1)
            eng.wait_ge(s, n)

        def wait_before(eng, what, step, back, turn):
            before = K.prev[what, step]
            if len(before) >= back:
                wait(eng, what, before[-back], turn)

        def bank(job):
            return work[K.bank[job]]

        def done(job):
            return ready[K.bank[job]]

        def freed(job):
            return free[K.bank[job]]

        def parts(eng, part):
            for b in range(-1, LOOP_FROM):
                part(b, None)
            with eng.Fori(0, (LOOP_TO - LOOP_FROM) // 2) as turn:
                for b in (LOOP_FROM, LOOP_FROM + 1):
                    part(b, turn)
            for b in range(LOOP_TO, B + 1):
                part(b, None)

        def row(b, turn):
            return b if turn is None else turn * 2 + b

        weight_loads = 13
        groups = 8 + 3 + 1 + 1 + 1 + 1 + 1

        block = ctx.enter_context(nc.Block())

        @block.sync
        def _(sp):
            for dst, src in (
                (st_g.bitcast(I32).rearrange("p (m e) -> p m e", m=HM), w_gate.rearrange("(m p) e -> p m e", p=P)),
                (st_u.bitcast(I32).rearrange("p (m e) -> p m e", m=HM), w_up.rearrange("(m p) e -> p m e", p=P)),
                (st_d.bitcast(I32).rearrange("p (h k) -> p h k", h=EH), w_down.rearrange("(h p) k -> p h k", p=P)),
                (st_z.rearrange("p (h e) -> p h e", h=EH), W_z.rearrange("(h p) e -> p h e", p=P)),
                (st_o.rearrange("p (h e) -> p h e", h=EH), W_out.rearrange("(h p) e -> p h e", p=P)),
                (st_p[0:R + 2 * N, :], W_params),
                (st_dt.rearrange("p (h r) -> p h r", h=EH), W_dt.rearrange("(h p) r -> p h r", p=P)),
                (a_coef[:], A_log.rearrange("(h p) n -> p h n", p=P)),
                (taps[:], conv_w.rearrange("(h p) o k -> p h (o k)", p=P)),
                (wdt_t[R:R + 1, :], b_dt.rearrange("(o e) -> o e", o=1)),
            ):
                sp.dma_start(dst, src).then_inc(w_landed, 16)
            with nc.allow_non_contiguous_dma(reason="256 numbers, one to a partition"):
                sp.dma_start(d_skip[:], D.rearrange("(h p) -> p h", p=P)).then_inc(w_landed, 16)

            def part(b, turn):
                for ev in steps(b):
                    if ev[0] == "ld":
                        _, bt, c = ev
                        wait(sp, "free", ("dn", 1, bt - 1, c, 1), turn)
                        src = x[row(bt, turn)].rearrange("(c j p) e -> c p j e", c=NC, p=P)[c]
                        sp.dma_start(x_in[:, c * TJ:(c + 1) * TJ, :], src).then_inc(S[f"ld{c}"], 16)
                    elif ev[0] == "st":
                        _, bt, c = ev
                        wait(sp, "free", ("dn", 2, bt, c, 1), turn)
                        dst = out[row(bt, turn)].rearrange("(c j p) e -> c p j e", c=NC, p=P)[c]
                        sp.dma_start(dst, x_fin[:, c * TJ:(c + 1) * TJ, :]).then_inc(S[f"st{c}"], 16)

            parts(sp, part)
            for c in range(NC):
                sp.wait_ge(S[f"st{c}"], 16 * B)

        @block.tensor
        def _(pe):
            pe.wait_ge(s_ident, 2)
            pe.wait_ge(w_set, 3)
            n = 0

            def turn_group(blocks):
                nonlocal n
                if n >= BANKS:
                    pe.wait_ge(w_kept, n - BANKS + 1)
                for i, src in enumerate(blocks):
                    k, m = src.shape
                    last = pe.transpose(work[n % BANKS][0:m, i * P:i * P + k], src, ident[0:k, 0:k])
                last.then_inc(w_turned, 1)
                n += 1

            for w in (st_g, st_u):
                for k in range(EH):
                    for m0 in (0, 4):
                        turn_group([w[:, m * E + k * P:m * E + (k + 1) * P] for m in range(m0, min(m0 + 4, HM))])
            for m0 in range(0, HM, 2):
                turn_group([st_d[:, h * HID + m * P:h * HID + (m + 1) * P] for m in (m0, m0 + 1) for h in range(EH)])
            for w in (st_z, st_o):
                turn_group([w[:, h * E + k * P:h * E + (k + 1) * P] for k in range(EH) for h in range(EH)])
            turn_group([st_p[0:R + 2 * N, k * P:(k + 1) * P] for k in range(EH)])
            turn_group([st_dt[:, h * R:(h + 1) * R] for h in range(EH)])
            pe.wait_ge(s_set, 1)
            turn_group([inv_a_u[:, h, :] for h in range(EH)])
            pe.matmul(c_bank[0:1, 0:EH * N], ones[:], tiny[:].rearrange("p h n -> p (h n)"), start=True,
                      stop=True).then_inc(s_flag, 1)
            pe.wait_ge(w_kept, groups)
            pe.wait_ge(s_flag, 3)

            def part(b, turn):
                def take(job):
                    s, n = K.at["free", job]
                    if n > 1:
                        n -= 1
                        pe.wait_ge(free[s], n if turn is None else turn * K.bank_slope + n)
                    return bank(job)

                for ev in steps(b):
                    kind = ev[0]
                    if kind == "T":
                        wait(pe, "normed", ("ln",) + ev[1:], turn)
                        for h in range(EH):
                            job = ev + (h,)
                            dst = take(job)
                            for j in range(TJ):
                                last = pe.transpose(dst[:, j * P:(j + 1) * P], normed[:, j, h * P:(h + 1) * P], ident[:])
                            last.then_inc(done(job), 1)
                    elif kind == "gu":
                        _, f, bt, c, m = ev
                        wait(pe, "free", ("T", 1 if f == 1 else 3, bt, c, EH - 1), turn)
                        for w, name in ((wg_t, "gate"), (wu_t, "up")):
                            job = ev + (name,)
                            dst = take(job)
                            for k in range(EH):
                                for i, part_ in enumerate((xt_hi[c], xt_lo[c])):
                                    last = pe.matmul(dst[:], w[:, k, m * P:(m + 1) * P], part_[:, k, :],
                                                     start=(k == 0 and i == 0), stop=(k == EH - 1 and i == 1))
                            last.then_inc(done(job), 1)
                    elif kind == "dn":
                        _, f, bt, c, jp = ev
                        wait(pe, "lo", ("hl", f, bt, c, HM - 1), turn)
                        dst = take(ev)
                        for j in range(2):
                            t = (2 * jp + j) * P
                            for m in range(HM):
                                for i, part_ in enumerate((hid_hi, hid_lo)):
                                    last = pe.matmul(dst[:, j * E:(j + 1) * E], part_[:, m, t:t + P], wd_t[:, m, :],
                                                     start=(m == 0 and i == 0), stop=(m == HM - 1 and i == 1))
                        last.then_inc(done(ev), 1)
                    elif kind == "op":
                        _, bt, jp = ev
                        wait(pe, "gated", ("gate", bt), turn)
                        dst = take(ev)
                        for j in range(2):
                            t = (2 * jp + j) * P
                            for h in range(EH):
                                last = pe.matmul(dst[:, j * E:(j + 1) * E], acc[bt % 2][:, h, t:t + P], wo_t[:, h, :],
                                                 start=(h == 0), stop=(h == EH - 1))
                        last.then_inc(done(ev), 1)
                    elif kind == "z":
                        _, bt, h, c = ev
                        dst = take(ev)
                        for k in range(EH):
                            last = pe.matmul(dst[:], wz_t[:, k, h * P:(h + 1) * P],
                                             xt[:, k, KW - 1 + c * CH:KW - 1 + (c + 1) * CH],
                                             start=(k == 0), stop=(k == EH - 1))
                        last.then_inc(done(ev), 1)
                    elif kind == "pm":
                        _, bt, c = ev
                        wait(pe, "free", ("T", 2, bt, c, EH - 2), turn)
                        wait(pe, "free", ("T", 2, bt, c, EH - 1), turn)
                        dst = take(ev)
                        for k in range(EH):
                            last = pe.matmul(dst[0:PROWS, :], wp_t[:, k, :],
                                             xt[:, k, KW - 1 + c * CH:KW - 1 + (c + 1) * CH],
                                             start=(k == 0), stop=(k == EH - 1))
                        last.then_inc(done(ev), 1)
                    elif kind == "cv":
                        _, bt, h, c = ev
                        dst = take(ev)
                        for k in range(KW):
                            last = pe.matmul(dst[:], tap_diag[:, h, k, :], xt[:, h, k + c * CH:k + (c + 1) * CH],
                                             start=(k == 0), stop=(k == KW - 1))
                        last.then_inc(done(ev), 1)
                    elif kind == "dt":
                        _, bt, h, c = ev
                        wait(pe, "c_high", ("pm", bt, c), turn)
                        dst = take(ev)
                        pe.matmul(dst[:], wdt_t[:, h * P:(h + 1) * P], params[0:R + 1, c * CH:(c + 1) * CH],
                                  start=True, stop=True).then_inc(done(ev), 1)
                    elif kind == "rm":
                        _, bt, h, c = ev
                        wait(pe, "c_high", ("pm", bt, c), turn)
                        dst = take(ev)
                        pe.matmul(dst[:], inv_a_t[CD_ROW:CD_ROW + N, h * P:(h + 1) * P],
                                  params[CD_ROW:CD_ROW + N, c * CH:(c + 1) * CH],
                                  start=True, stop=True).then_inc(done(ev), 1)
                    elif kind == "bc":
                        _, bt, s = ev
                        wait(pe, "free", ("pm", bt, NC - 1), turn)
                        if s:
                            wait(pe, "weighted", ("cm", bt, s - 1, EH - 1), turn)
                        else:
                            wait(pe, "weighted", ("cm", bt - 1, N - 1, EH - 1), turn)
                        for c in range(NC):
                            last = pe.matmul(c_bank[:, c * CH:(c + 1) * CH], pick[C_ROW:P, s:s + 1].to_broadcast([P - C_ROW, P]),
                                             c_parts[bt % 2][C_ROW:P, c * CH:(c + 1) * CH], start=True, stop=True)
                        last.then_inc(S["c_spread"], 1)

            parts(pe, part)

        @block.scalar
        def _(act):
            act.wait_ge(w_landed, 16 * 11)
            nc.scalar.activation(a_coef[:], a_coef[:], ACT.Exp).then_inc(s_exp, 1)
            act.wait_ge(w_kept, groups)
            act.wait_ge(s_set, 1)

            def part(b, turn):
                for ev in steps(b):
                    kind = ev[0]
                    if kind == "ln":
                        _, f, bt, c = ev
                        slot = K.at["meanvar", ev][1] % 2
                        src = {1: x_in, 2: x_mid[bt % 2], 3: x_fin}[f]
                        wait(act, "ready", K.was[ev], turn)
                        wait(act, "rstd", ev, turn)
                        for j in range(TJ):
                            last = nc.scalar.activation(normed[:, j, :], src[:, c * TJ + j, :], ACT.Identity,
                                                        bias=shift[:, slot, j:j + 1], scale=rstd[:, slot, j:j + 1])
                        last.then_inc(S["normed"], 1)
                    elif kind == "T":
                        _, f, bt, c = ev
                        for h in range(EH):
                            job = ev + (h,)
                            wait(act, "ready", job, turn)
                            if f == 2:
                                if h == 0:
                                    wait(act, "ready", ("z", bt - 1, EH - 1, NC - 1), turn)
                                nc.scalar.activation(xt[:, h, KW - 1 + c * CH:KW - 1 + (c + 1) * CH], bank(job)[:],
                                                     ACT.Copy).then_inc(freed(job), 1)
                            else:
                                if h == 0:
                                    wait(act, "ready", K.was[ev], turn)
                                nc.scalar.activation(xt_hi[c][:, h, :], bank(job)[:], ACT.Copy).then_inc(S["xhi"], 1)
                    elif kind in ("gu", "z", "cv"):
                        job = ev + ("gate",) if kind == "gu" else ev
                        wait(act, "ready", job, turn)
                        before = K.prev["tanh", ev]
                        if len(before) == TANHS:
                            was = before[0]
                            wait(act, "free", was + ("gate",) if was[0] == "gu" else was, turn)
                        slot = K.at["tanh", ev][1] % TANHS
                        nc.scalar.activation(tanh[:, slot, :], bank(job)[:], ACT.Tanh,
                                             scale=GATE_HALF if kind == "gu" else 0.5).then_inc(S["tanh"], 1)
                    elif kind == "hl":
                        _, f, bt, c, m = ev
                        wait(act, "free", ("gu",) + ev[1:] + ("up",), turn)
                        if m == 0:
                            wait(act, "ready", K.was[ev], turn)
                        slot = K.at["hi", ev][1] % 2
                        nc.scalar.activation(hid_hi[:, m, :], hid[:, slot, :], ACT.Copy).then_inc(S["hi"], 1)
                    elif kind == "pm":
                        _, bt, c = ev
                        wait(act, "ready", ev, turn)
                        wait(act, "ready", ("rm", bt - 1, EH - 1, c), turn)
                        wait(act, "c_spread", ("bc", bt - 2, N - 1), turn)
                        src, t = bank(ev), slice(c * CH, (c + 1) * CH)
                        nc.scalar.activation(params[0:R, t], src[0:R, :], ACT.Copy)
                        nc.scalar.activation(params[CD_ROW:CD_ROW + N, t], src[CD_ROW:CD_ROW + N, :], ACT.Copy)
                        nc.scalar.activation(c_parts[bt % 2][C_ROW:C_ROW + N, t], src[C_ROW:C_ROW + N, :], ACT.Copy)
                        nc.scalar.activation(c_parts[bt % 2][CD_ROW:CD_ROW + N, t], src[CD_ROW:CD_ROW + N, :],
                                             ACT.Copy).then_inc(S["c_high"], 1)
                    elif kind == "dt":
                        _, bt, h, c = ev
                        wait(act, "ready", ev, turn)
                        wait(act, "scanned", ("scan", bt - 2, N - 1, EH - 1), turn)
                        y = dt[bt % 2][:, h, 1 + c * CH:1 + (c + 1) * CH]
                        nc.scalar.activation(y, bank(ev)[:], ACT.Abs).then_inc(S["sp_exp"], 1)
                        wait(act, "sp_exp", ev, turn, less=1)
                        nc.scalar.activation(y, y, ACT.Exp, scale=-1.0).then_inc(S["sp_exp"], 1)
                    elif kind == "ln1p":
                        _, bt, h, c = ev
                        wait(act, "sp_exp", ("dt", bt, h, c), turn)
                        wait(act, "sp_sum", ("dts", bt, h - 1, c) if h else ("dts", bt - 1, EH - 1, c), turn)
                        nc.scalar.activation(sp_l[:, c, :], dt[bt % 2][:, h, 1 + c * CH:1 + (c + 1) * CH], ACT.Ln,
                                             bias=1.0).then_inc(S["sp_ln"], 1)
                    elif kind == "scan":
                        _, bt, s, h = ev
                        if s == 0 and h == 0:
                            wait(act, "dt_first", ("dt0", bt), turn)
                        wait_before(act, "scanned", ev, 2, turn)
                        slot = K.at["decay", ev][1] % 2
                        nc.scalar.activation(decay[:, slot, :], dt[bt % 2][:, h, 0:L], ACT.Exp,
                                             scale=a_coef[:, h, s:s + 1]).then_inc(S["decay"], 1)

            parts(act, part)

        @block.gpsimd
        def _(pool):
            nc.gpsimd.memset(ident[:], 0.0).then_inc(s_ident, 1)
            pool.wait_ge(s_ident, 1)
            nc.gpsimd.affine_select(out=ident[:], in_=ident[:], compare_op=ALU.not_equal, fill=1.0, base=0,
                                    pattern=[[-1, P]], channel_multiplier=1).then_inc(s_ident, 1)
            pool.wait_ge(w_kept, groups)
            pool.wait_ge(s_set, 1)
            def part(b, turn):
                for ev in steps(b):
                    kind = ev[0]
                    if kind == "ln":
                        _, f, bt, c = ev
                        slot = K.at["meanvar", ev][1] % 2
                        r = rstd[:, slot, :]
                        wait_before(pool, "normed", ev, 2, turn)
                        wait(pool, "meanvar", ev, turn)
                        nc.gpsimd.tensor_tensor(r, meanvar[:, slot, :, 1], eps[:], ALU.add).then_inc(S["rstd"], 1)
                        wait(pool, "rstd", ev, turn, less=4)
                        nc.gpsimd.tensor_tensor(r, r, minus_half[:], ALU.pow).then_inc(S["rstd"], 1)
                        wait(pool, "rstd", ev, turn, less=3, apart=True)
                        nc.gpsimd.tensor_scalar(r, r, -1.0 if f == 2 else -XS, None, ALU.mult).then_inc(S["rstd"], 1)
                        wait(pool, "rstd", ev, turn, less=2)
                        nc.gpsimd.tensor_tensor(shift[:, slot, :], meanvar[:, slot, :, 0], r, ALU.mult).then_inc(S["rstd"], 1)
                        nc.gpsimd.tensor_scalar(r, r, -1.0, None, ALU.mult).then_inc(S["rstd"], 1)
                    elif kind == "hl":
                        m = ev[4]
                        wait(pool, "hi", ev, turn)
                        slot = K.at["hi", ev][1] % 2
                        nc.gpsimd.tensor_tensor(hid_lo[:, m, :], hid[:, slot, :], hid_hi[:, m, :],
                                                ALU.subtract).then_inc(S["lo"], 1)
                    elif kind == "dts":
                        _, bt, h, c = ev
                        y = dt[bt % 2][:, h, 1 + c * CH:1 + (c + 1) * CH]
                        wait_before(pool, "sp_sum", ev, 1, turn)
                        wait(pool, "sp_ln", ("ln1p", bt, h, c), turn, apart=True)
                        nc.gpsimd.tensor_scalar(sp_v[:], y, 1.0, 1.0, ALU.add, ALU.subtract).then_inc(S["sp_sum"], 1)
                        wait(pool, "sp_sum", ev, turn, less=2)
                        nc.gpsimd.tensor_tensor(sp_l[:, c, :], sp_l[:, c, :], sp_v[:], ALU.subtract).then_inc(S["sp_sum"], 1)
                        wait(pool, "sp_sum", ev, turn, less=1)
                        nc.gpsimd.tensor_tensor(y, sp_l[:, c, :], y, ALU.add).then_inc(S["sp_sum"], 1)
                    elif kind == "cm":
                        _, bt, s, h = ev
                        if s == 0 and h == 0:
                            wait(pool, "acc_begun", ("ai", bt, EH - 1, NC - 1), turn)
                        wait(pool, "weighted", ev, turn)
                        wait_before(pool, "summed", ev, 2, turn)
                        slot = K.at["weighted", ev][1] % 2
                        nc.gpsimd.tensor_tensor(acc[bt % 2][:, h, :], acc[bt % 2][:, h, :], cg[:, slot, :],
                                                ALU.add).then_inc(S["summed"], 1)
                    elif kind == "d":
                        _, bt, h = ev
                        if h == 0:
                            wait(pool, "u_first", ("u0", bt), turn)
                        wait(pool, "scanned", ("scan", bt - 1, N - 1, h), turn)
                        nc.gpsimd.tensor_tensor(du[:, h, :], u[bt % 2][:, h, 1:1 + L], u[bt % 2][:, h, 0:L],
                                                ALU.subtract).then_inc(S["du"], 1)

            parts(pool, part)

        @block.vector
        def _(dve):
            own = 0

            def then(ins):
                nonlocal own
                own += 1
                ins.then_inc(w_set, 1)
                dve.wait_ge(w_set, own)

            dve.wait_ge(w_landed, 16 * 11)
            for w in (st_g, st_u, st_d):
                then(nc.vector.tensor_copy(w, w.bitcast(I32)))
            for t in (wp_t[:], inv_a_u, pick[:].bitcast(F32), c_parts[0][:].bitcast(F32), c_parts[1][:].bitcast(F32),
                      xt[:, :, 0:KW - 1], u[0][:, :, 0:1], u[1][:, :, 0:1], params[C_ROW:P, :]):
                then(nc.vector.memset(t, 0.0))
            then(nc.vector.memset(ones[:], 1.0))
            then(nc.vector.memset(minus_half[:], -0.5))
            then(nc.vector.memset(eps[:], EPS))
            then(nc.vector.memset(params[R:R + 1, :], 1.0))
            dve.wait_ge(s_ident, 2)
            then(nc.vector.tensor_copy(pick[C_ROW:C_ROW + N, :], ident[C_ROW:C_ROW + N, C_ROW:C_ROW + N]))
            then(nc.vector.tensor_copy(pick[CD_ROW:CD_ROW + N, :], ident[CD_ROW:CD_ROW + N, CD_ROW:CD_ROW + N]))
            for h in range(EH):
                for k in range(KW):
                    then(nc.vector.tensor_scalar(tap_diag[:, h, k, :], ident[:], taps[:, h, k:k + 1], None, ALU.mult))
            dve.wait_ge(s_exp, 1)
            then(nc.vector.tensor_scalar(tiny[:], a_coef[:], A_MIN, None, ALU.is_lt))
            then(nc.vector.tensor_scalar(a_coef[:], a_coef[:], -1.0, None, ALU.mult))
            then(nc.vector.tensor_scalar(kept[:], tiny[:], -1.0, 1.0, ALU.mult, ALU.add))
            then(nc.vector.scalar_tensor_tensor(inv_a[:], a_coef[:], 1e-10, kept[:], ALU.add, ALU.mult))
            then(nc.vector.tensor_tensor(inv_a[:], inv_a[:], tiny[:], ALU.subtract))
            then(nc.vector.reciprocal(inv_a[:], inv_a[:]))
            then(nc.vector.tensor_tensor(inv_a[:], inv_a[:], kept[:], ALU.mult))
            then(nc.vector.tensor_copy(inv_a_u[:, :, CD_ROW:CD_ROW + N], inv_a[:]))
            then(nc.vector.tensor_tensor(inv_a[:], inv_a[:], tiny[:], ALU.add))
            nc.vector.tensor_copy(flag_f[:], ones[0:1, :]).then_inc(s_set, 1)
            n = 0

            def keep(copies):
                nonlocal n
                dve.wait_ge(w_turned, n + 1)
                for dst, src in copies(work[n % BANKS]):
                    last = nc.vector.tensor_copy(dst, src)
                last.then_inc(w_kept, 1)
                n += 1

            for w in (wg_t, wu_t):
                for k in range(EH):
                    for m0, m1 in ((0, 4), (4, HM)):
                        keep(lambda ps: [(w[:, k, m0 * P:m1 * P], ps[:, 0:(m1 - m0) * P])])
            for m0 in range(0, HM, 2):
                keep(lambda ps: [(wd_t[:, m0:m0 + 2, :].rearrange("p m e -> p (m e)"), ps[:])])
            for w in (wz_t, wo_t):
                keep(lambda ps: [(w[:].rearrange("p k e -> p (k e)"), ps[:])])
            keep(lambda ps: [(wp_t[:, k, a:a + m], ps[:, k * P + o:k * P + o + m]) for k in range(EH)
                             for a, o, m in ((0, 0, R), (C_ROW, R + N, N), (CD_ROW, R + N, N))])
            keep(lambda ps: [(wdt_t[0:R, :], ps[0:R, 0:E])])
            keep(lambda ps: [(inv_a_t[CD_ROW:CD_ROW + N, :], ps[CD_ROW:CD_ROW + N, 0:E])])
            dve.wait_ge(s_flag, 1)
            nc.vector.tensor_reduce(flag_f[:], c_bank[0:1, 0:EH * N], AX_X, ALU.add).then_inc(s_flag, 1)
            dve.wait_ge(s_flag, 2)
            nc.vector.tensor_copy(flag[:], flag_f[:]).then_inc(s_flag, 1)
            dve.wait_ge(s_flag, 3)
            dve.wait_ge(w_kept, groups)
            n_tiny = dve.value_load(flag[0:1, 0:1])

            def program(with_tiny):
                def part(b, turn):
                    for ev in steps(b):
                        kind = ev[0]
                        if kind == "ln":
                            _, f, bt, c = ev
                            slot = K.at["meanvar", ev][1] % 2
                            src = {1: x_in, 2: x_mid[bt % 2], 3: x_fin}[f]
                            if f == 1:
                                wait(dve, f"ld{c}", ("ld", bt, c), turn)
                            elif f == 2:
                                wait(dve, "free", ("dn", 1, bt, c, 1), turn)
                            else:
                                wait(dve, "free", ("op", bt, 2 * c + 1), turn)
                            wait_before(dve, "normed", ev, 2, turn)
                            for j in range(TJ):
                                last = nc.vector.bn_stats(stats[:, slot, j, :], src[:, c * TJ + j, :])
                            last.then_inc(S["stats"], 1)
                            wait(dve, "stats", ev, turn, apart=True)
                            for j in range(TJ):
                                last = nc.vector.bn_aggr(meanvar[:, slot, j, :], stats[:, slot, j, :])
                            last.then_inc(S["meanvar"], 1)
                        elif kind == "Tl":
                            _, f, bt, c = ev
                            for h in range(EH):
                                job = ("T",) + ev[1:] + (h,)
                                if h == 0:
                                    wait(dve, "xhi", ("T",) + ev[1:], turn)
                                nc.vector.tensor_tensor(xt_lo[c][:, h, :], bank(job)[:], xt_hi[c][:, h, :],
                                                        ALU.subtract).then_inc(freed(job), 1)
                        elif kind == "sh":
                            gu = ("gu",) + ev[1:]
                            wait(dve, "tanh", gu, turn)
                            i = K.at["hi", ("hl",) + ev[1:]][1] % 2
                            wait_before(dve, "lo", ("hl",) + ev[1:], 2, turn)
                            nc.vector.scalar_tensor_tensor(hid[:, i, :], tanh[:, K.at["tanh", gu][1] % TANHS, :], 1.0,
                                                           bank(gu + ("gate",))[:], ALU.add,
                                                           ALU.mult).then_inc(freed(gu + ("gate",)), 1)
                            wait(dve, "free", gu + ("gate",), turn)
                            wait(dve, "ready", gu + ("up",), turn)
                            nc.vector.scalar_tensor_tensor(hid[:, i, :], hid[:, i, :], H_SCALE, bank(gu + ("up",))[:],
                                                           ALU.mult, ALU.mult).then_inc(freed(gu + ("up",)), 1)
                        elif kind == "rs":
                            _, f, bt, c, jp = ev
                            job = ("dn",) + ev[1:]
                            t = slice(c * TJ + 2 * jp, c * TJ + 2 * jp + 2)
                            src, dst = (x_in, x_mid[bt % 2]) if f == 1 else (x_fin, x_fin)
                            wait(dve, "ready", job, turn)
                            nc.vector.scalar_tensor_tensor(
                                dst[:, t, :].rearrange("p j e -> p (j e)"), bank(job)[:], OUT_SCALE,
                                src[:, t, :].rearrange("p j e -> p (j e)"), ALU.mult, ALU.add).then_inc(freed(job), 1)
                        elif kind == "ra":
                            _, bt, jp = ev
                            job = ("op", bt, jp)
                            t = slice(2 * jp, 2 * jp + 2)
                            wait(dve, f"st{jp // 2}", ("st", bt - 1, jp // 2), turn)
                            wait(dve, "ready", job, turn)
                            nc.vector.tensor_tensor(
                                x_fin[:, t, :].rearrange("p j e -> p (j e)"), bank(job)[:],
                                x_mid[bt % 2][:, t, :].rearrange("p j e -> p (j e)"), ALU.add).then_inc(freed(job), 1)
                        elif kind == "gate":
                            _, bt = ev
                            wait(dve, "summed", ("cm", bt, N - 1, EH - 1), turn)
                            for h in range(EH):
                                nc.vector.scalar_tensor_tensor(acc[bt % 2][:, h, :], acc[bt % 2][:, h, :], 0.25, zs[:, h, :],
                                                               ALU.mult, ALU.mult).then_inc(S["gated"], 1)
                        elif kind == "zs":
                            _, bt, h, c = ev
                            job = ("z",) + ev[1:]
                            wait(dve, "tanh", job, turn)
                            wait(dve, "gated", ("gate", bt - 1), turn)
                            nc.vector.scalar_tensor_tensor(zs[:, h, c * CH:(c + 1) * CH], tanh[:, K.at["tanh", job][1] % TANHS, :], 1.0,
                                                           bank(job)[:], ALU.add, ALU.mult).then_inc(freed(job), 1)
                        elif kind == "pl":
                            _, bt = ev
                            for c in range(NC):
                                job = ("pm", bt, c)
                                wait(dve, "c_high", job, turn)
                                low = c_parts[bt % 2][CD_ROW:CD_ROW + N, c * CH:(c + 1) * CH]
                                nc.vector.tensor_tensor(low, bank(job)[CD_ROW:CD_ROW + N, :], low.bitcast(F32),
                                                        ALU.subtract).then_inc(freed(job), 1)
                        elif kind == "us":
                            _, bt, h, c = ev
                            job = ("cv",) + ev[1:]
                            wait(dve, "tanh", job, turn)
                            wait(dve, "du", ("d", bt - 2, EH - 1), turn)
                            nc.vector.scalar_tensor_tensor(u[bt % 2][:, h, 2 + c * CH:2 + (c + 1) * CH],
                                                           tanh[:, K.at["tanh", job][1] % TANHS, :], 1.0, bank(job)[:],
                                                           ALU.add, ALU.mult).then_inc(freed(job), 1)
                        elif kind == "u0":
                            _, bt = ev
                            wait(dve, "free", ("cv", bt, EH - 1, 0), turn)
                            nc.vector.tensor_copy(u[bt % 2][:, :, 1:2], u[bt % 2][:, :, 2:3]).then_inc(S["u_first"], 1)
                        elif kind == "dr":
                            _, bt, h, c = ev
                            job = ("dt",) + ev[1:]
                            wait(dve, "sp_exp", job, turn, less=1)
                            wait(dve, "sp_added", ("dtf", bt, h - 1, c) if h else ("dtf", bt - 1, EH - 1, c), turn)
                            nc.vector.tensor_scalar(sp_r[:, c, :], bank(job)[:], 0.0, None, ALU.max).then_inc(freed(job), 1)
                        elif kind == "dtf":
                            _, bt, h, c = ev
                            y = dt[bt % 2][:, h, 1 + c * CH:1 + (c + 1) * CH]
                            wait(dve, "free", ("dt",) + ev[1:], turn)
                            wait(dve, "sp_sum", ("dts",) + ev[1:], turn)
                            nc.vector.tensor_tensor(y, sp_r[:, c, :], y, ALU.add).then_inc(S["sp_added"], 1)
                        elif kind == "dt0":
                            _, bt = ev
                            for h in range(EH):
                                wait(dve, "sp_added", ("dtf", bt, h, 0), turn)
                            nc.vector.tensor_copy(dt[bt % 2][:, :, 0:1], dt[bt % 2][:, :, 1:2]).then_inc(S["dt_first"], 1)
                        elif kind == "ai":
                            _, bt, h, c = ev
                            job = ("rm",) + ev[1:]
                            t = acc[bt % 2][:, h, c * CH:(c + 1) * CH]
                            wait(dve, "ready", job, turn)
                            wait(dve, "u_first", ("u0", bt), turn)
                            nc.vector.tensor_tensor(t, bank(job)[:], u[bt % 2][:, h, 1 + c * CH:1 + (c + 1) * CH],
                                                    ALU.mult).then_inc(freed(job), 1)
                            wait(dve, "free", job, turn)
                            nc.vector.scalar_tensor_tensor(t, u[bt % 2][:, h, 2 + c * CH:2 + (c + 1) * CH], d_skip[:, h:h + 1], t,
                                                           ALU.mult, ALU.subtract).then_inc(S["acc_begun"], 1)
                        elif kind == "scan":
                            _, bt, s, h = ev
                            i = K.at["scanned", ev][1] % 2
                            if s == 0:
                                wait(dve, "du", ("d", bt, h), turn)
                            wait(dve, "decay", ev, turn)
                            was = K.prev["scanned", ev][-2:]
                            if len(was) == 2:
                                wait(dve, "weighted", ("cm",) + was[0][1:], turn)
                            scan = nc.vector.tensor_tensor_scan(g[:, i, :], du[:, h, :], decay[:, i, :], 0.0, ALU.add, ALU.mult)
                            if not with_tiny:
                                scan.then_inc(S["scanned"], 1)
                                continue
                            _, k = K.at["scanned", ev]
                            at = 4 * (k - 1) if turn is None else turn * (4 * K.slope["scanned"]) + 4 * (k - 1)
                            scan.then_inc(s_fix, 1)
                            if len(was) == 2:
                                wait(dve, "summed", ("cm",) + was[0][1:], turn)
                            v = cg[:, i, :]
                            nc.vector.scalar_tensor_tensor(v, dt[bt % 2][:, h, 0:L], tiny[:, h, s:s + 1], u[bt % 2][:, h, 1:1 + L],
                                                           ALU.mult, ALU.mult).then_inc(s_fix, 1)
                            dve.wait_ge(s_fix, at + 2)
                            nc.vector.tensor_tensor_scan(v, decay[:, i, :], v, 0.0, ALU.mult, ALU.add).then_inc(s_fix, 1)
                            dve.wait_ge(s_fix, at + 3)
                            nc.vector.tensor_scalar(g[:, i, :], g[:, i, :], kept[:, h, s:s + 1], None, ALU.mult).then_inc(s_fix, 1)
                            dve.wait_ge(s_fix, at + 4)
                            nc.vector.tensor_tensor(g[:, i, :], g[:, i, :], v, ALU.add).then_inc(S["scanned"], 1)
                        elif kind == "cm":
                            _, bt, s, h = ev
                            i = K.at["weighted", ev][1] % 2
                            wait(dve, "scanned", ("scan",) + ev[1:], turn)
                            wait(dve, "c_spread", ("bc", bt, s), turn)
                            was = K.prev["weighted", ev][-2:]
                            if len(was) == 2:
                                wait(dve, "summed", was[0], turn)
                            nc.vector.scalar_tensor_tensor(cg[:, i, :], g[:, i, :], inv_a[:, h, s:s + 1], c_bank[:],
                                                           ALU.mult, ALU.mult).then_inc(S["weighted"], 1)

                parts(dve, part)

            with dve.If(n_tiny > 0):
                program(True)
            with dve.Else():
                program(False)


INS = ("L0_attn_x", "L0_attn_W_z", "L0_attn_W_params", "L0_attn_conv_w", "L0_attn_W_dt", "L0_attn_b_dt", "L0_attn_A_log",
       "L0_attn_D", "L0_attn_W_out", "L0_ffn_w_gate", "L0_ffn_w_up", "L0_ffn_w_down")


def kernel(**inputs):
    import concourse.bacc as bacc
    from concourse.bass_utils import run_bass_kernel_spmd

    nc = bacc.Bacc("TRN2", target_bir_lowering=False, num_devices=1)
    arrays, args = {}, []
    for name in INS:
        a = np.ascontiguousarray(inputs[name])
        arrays[name] = a
        args.append(nc.dram_tensor(name, a.shape, mybir.dt.from_np(a.dtype), kind="ExternalInput").ap())
    out = nc.dram_tensor("out", (B, L, E), F32, kind="ExternalOutput").ap()
    macaron_kernel(nc, *args, out)
    return run_bass_kernel_spmd(nc, [arrays], core_ids=[0]).results[0]["out"]
```

```python
from contextlib import ExitStack

import numpy as np

import concourse.bass as bass
from concourse import mybir

ALU = mybir.AluOpType
ACT = mybir.ActivationFunctionType
AX_X = mybir.AxisListType.X
F32 = mybir.dt.float32
F32R = mybir.dt.float32r
F16 = mybir.dt.float16
I32 = mybir.dt.int32

P = 128
B, L, E = 16, 1024, 256
HID = 768
N, KW, R = 16, 4, 64
EH = E // P
CH = 512
NC = L // CH
TJ = CH // P
HM = HID // P
AHEAD, DECAYS = 2, 4
HIDS = 3
TANHS = 4
BANKS = 6
EPS = 1e-5
A_MIN = 1e-5
XS = 1024.0
Q = 127.0
GATE_HALF = 0.5 / (XS * Q)
H_SCALE = 0.25 / (XS * Q) ** 2
OUT_SCALE = 1.0 / Q
C_ROW, CD_ROW = 64, 96
PROWS = CD_ROW + N
LOOP_FROM, LOOP_TO = 2, 14


def steps(b):
    ssm, ffn1, ffn2, ln1 = 0 <= b < B, 0 <= b + 1 < B, 0 <= b - 1 < B, 1 <= b + 2 < B
    at = {q: [] for q in range(2 * N + 4)}

    def put(q, *ev):
        at[q].append(ev)

    def rows(q, lag, f, bt, c):
        put(q, "ln", f, bt, c)
        put(q, "lr", f, bt, c)
        put(q + lag, "lx", f, bt, c)

    def turned(q, f, bt, c):
        put(q, "T", f, bt, c)
        put(q, "Te", f, bt, c)
        if f != 2:
            put(q + 1, "Tl", f, bt, c)

    def hidden(f, bt, q0):
        for c in range(NC):
            for m in range(HM):
                q = q0 + c * (HM + 1) + m
                put(q, "gu", f, bt, c, m)
                put(q, "th", "gu", f, bt, c, m)
                put(q + 1, "sh", f, bt, c, m)
                put(q + 2, "hi", f, bt, c, m)
                put(q + 2, "lo", f, bt, c, m)

    def down(f, bt, c, q):
        for jp in range(2):
            put(q, "dn", f, bt, c, jp)
            put(q + 1, "rs", f, bt, c, jp)

    out = []
    if b == -1:
        for c in range(NC):
            out += [("ld", 0, c)] + [(k, 1, 0, c) for k in ("ln", "lr", "lx", "T", "Te", "Tl")]
    if ffn2:
        put(2, "gate", b - 1)
        for jp in range(2 * NC):
            put(3, "op", b - 1, jp)
            put(4, "ra", b - 1, jp)
        down(2, b - 1, 0, 22)
        down(2, b - 1, 1, 29)
        rows(6, 1, 3, b - 1, 0)
        turned(9, 3, b - 1, 0)
        rows(12, 1, 3, b - 1, 1)
        turned(15, 3, b - 1, 1)
    if ffn1:
        down(1, b + 1, 0, 8)
        down(1, b + 1, 1, 15)
        rows(10, 1, 2, b + 1, 0)
        turned(12, 2, b + 1, 0)
        rows(16, 1, 2, b + 1, 1)
        turned(18, 2, b + 1, 1)
        for c in range(NC):
            put(19, "pm", b + 1, c)
            put(20, "pe", b + 1, c)
        put(21, "pl", b + 1)
        for c in range(NC):
            for h in range(EH):
                put(20 + c, "cv", b + 1, h, c)
                put(20 + c, "th", "cv", b + 1, h, c)
                put(21 + c, "us", b + 1, h, c)
        put(23, "u0", b + 1)
        for h in range(EH):
            for kind, q in (("dt", 22), ("da", 22), ("dl", 23), ("dp", 24), ("df", 25)):
                for c in range(NC):
                    put(q + 2 * h, kind, b + 1, h, c)
        put(28, "dt0", b + 1)
        for h in range(EH):
            for c in range(NC):
                put(25 + h, "rm", b + 1, h, c)
                put(26 + h, "ai", b + 1, h, c)
    if ln1:
        for c in range(NC):
            put(17, "ld", b + 2, c)
        rows(21, 1, 1, b + 2, 0)
        turned(24, 1, b + 2, 0)
        rows(27, 1, 1, b + 2, 1)
        turned(30, 1, b + 2, 1)
    if ssm:
        for c in range(NC):
            for h in range(EH):
                put(4 + c, "z", b, h, c)
                put(4 + c, "th", "z", b, h, c)
                put(5 + c, "zs", b, h, c)
    if ffn1:
        hidden(1, b + 1, 0)
    if ffn2:
        hidden(2, b - 1, 14)
    for q in range(2 * N + 4):
        row, slot = (b, q + AHEAD) if q + AHEAD < 2 * N else (b + 1, q + AHEAD - 2 * N)
        if q < 2 * N and 0 <= row < B:
            out.append(("ex", row, slot // EH, slot % EH))
        if ssm and q < 2 * N:
            out.append(("scan", b, q // EH, q % EH))
        out += at[q]
        if ssm and q < 2 * N:
            if q:
                out.append(("cm", b, (q - 1) // EH, (q - 1) % EH))
            if q % EH == 0:
                out.append(("bc", b, q // EH))
        if ssm and q == 2 * N - 1:
            out.append(("cm", b, N - 1, EH - 1))
    if ffn1:
        for h in range(EH):
            out.append(("d", b + 1, h))
    if ffn2:
        for c in range(NC):
            out.append(("st", b - 1, c))
    return out


class Counts:

    def __init__(self):
        self.at, self.bank, self.prev, self.total, self.was = {}, {}, {}, {}, {}
        last = {}
        self.slope = {}
        count, jobs, order = {}, 0, {}
        for b in range(-1, B + 1):
            for ev in steps(b):
                kind = ev[0]
                if kind == "T" and ev[1] != 2:
                    self.was[ev] = last.get(("gu", ev[3]))
                elif kind == "hi":
                    self.was[ev] = last.get("dn")
                elif kind == "lx":
                    self.was[ev] = last.get("T")
                if kind in ("lx", "T"):
                    assert last.get("row", "T") != kind, "rows are normalised and transposed in turns"
                    last["row"] = kind
                if kind == "gu":
                    last["gu", ev[3]] = ev + ("up",)
                elif kind == "dn":
                    last["dn"] = ev
                elif kind == "T":
                    last["T"] = ev + (EH - 1,)
                for job in self.jobs(ev):
                    k = jobs % BANKS
                    self.bank[job] = k
                    self.at["ready", job] = self.at["free", job] = (k, jobs // BANKS + 1)
                    jobs += 1
                for sem, n in self.increments(ev):
                    for i in range(n):
                        count[sem] = count.get(sem, 0) + 1
                    self.at[sem, ev] = (sem, count[sem])
                    before = order.setdefault(sem, [])
                    self.prev[sem, ev] = list(before[-TANHS:])
                    before.append(ev)
            self.total[b] = dict(count, jobs=jobs)
        one, two = self.total[LOOP_FROM - 1], self.total[LOOP_FROM + 1]
        self.slope = {s: two[s] - one[s] for s in two if s != "jobs"}
        assert (two["jobs"] - one["jobs"]) % BANKS == 0
        self.bank_slope = (two["jobs"] - one["jobs"]) // BANKS

    @staticmethod
    def jobs(ev):
        kind = ev[0]
        if kind == "gu":
            return [ev + ("gate",), ev + ("up",)]
        if kind == "T":
            return [ev + (h,) for h in range(EH)]
        return [ev] if kind in ("dn", "op", "z", "pm", "cv", "dt", "rm") else []

    @staticmethod
    def increments(ev):
        kind = ev[0]
        if kind == "ln":
            return [("stats", 1), ("meanvar", 1)]
        if kind == "Te":
            return [("xhi", EH)] if ev[1] != 2 else []
        if kind == "cm":
            return [("weighted", 1), ("summed", 1)]
        one = {"bc": "c_spread", "gate": "gated", "pe": "c_high", "u0": "u_first", "dt0": "dt_first", "ai": "acc_begun",
               "d": "du", "da": "sp_exp", "dl": "sp_ln", "dp": "sp_sum", "df": "sp_added", "th": "tanh", "hi": "hi",
               "lo": "lo", "lr": "rstd", "lx": "normed", "ex": "decay", "scan": "scanned"}
        if kind in one:
            return [(one[kind], {"gate": EH, "da": 2, "dp": 3, "lr": 4}.get(kind, 1))]
        if kind in ("ld", "st"):
            return [(f"{kind}{ev[2]}", 16)]
        return []


def macaron_kernel(nc, x, W_z, W_params, conv_w, W_dt, b_dt, A_log, D, W_out, w_gate, w_up, w_down, out):
    K = Counts()

    with ExitStack() as ctx:
        def sb(name, shape, dt=F32):
            return ctx.enter_context(nc.sbuf_tensor(name, shape, dt))

        def sem(name):
            return ctx.enter_context(nc.semaphore(name))

        x_in = sb("x_in", [P, NC * TJ, E])
        x_mid = [sb(f"x_mid{i}", [P, NC * TJ, E]) for i in range(2)]
        x_fin = sb("x_fin", [P, NC * TJ, E])
        normed = sb("normed", [P, TJ, E])
        stats = sb("stats", [P, 2, TJ, 6])
        meanvar = sb("meanvar", [P, 2, TJ, 2])
        rstd = sb("rstd", [P, 2, TJ])
        shift = sb("shift", [P, 2, TJ])
        xt_hi = [sb(f"xt_hi{i}", [P, EH, CH], F16) for i in range(2)]
        xt_lo = [sb(f"xt_lo{i}", [P, EH, CH], F16) for i in range(2)]
        xt = sb("xt", [P, EH, KW - 1 + L])
        tanh = sb("tanh", [P, TANHS, CH])
        hid = sb("hid", [P, HIDS, CH])
        hid_hi = sb("hid_hi", [P, HM, CH], F16)
        hid_lo = sb("hid_lo", [P, HM, CH], F16)
        zs = sb("zs", [P, EH, L])
        u = [sb(f"u{i}", [P, EH, 2 + L]) for i in range(2)]
        du = sb("du", [P, EH, L])
        dt = [sb(f"dt{i}", [P, EH, 1 + L]) for i in range(2)]
        params = sb("params", [P, L])
        c_parts = [sb(f"c_parts{i}", [P, L], F32R) for i in range(2)]
        ring = sb("ring", [P, DECAYS + 4, L])
        decay, g, cg = ring[:, 0:DECAYS, :], ring[:, DECAYS:DECAYS + 2, :], ring[:, DECAYS + 2:DECAYS + 4, :]
        acc = [sb(f"acc{i}", [P, EH, L]) for i in range(2)]
        sp_l = sb("sp_l", [P, 2, CH])
        sp_r = sb("sp_r", [P, 2, CH])
        sp_v = sb("sp_v", [P, CH])
        wg_t = sb("wg_t", [P, EH, HID], F16)
        wu_t = sb("wu_t", [P, EH, HID], F16)
        wd_t = sb("wd_t", [P, HM, E], F16)
        wz_t = sb("wz_t", [P, EH, E])
        wp_t = sb("wp_t", [P, EH, PROWS])
        wdt_t = sb("wdt_t", [R + 1, E])
        wo_t = sb("wo_t", [P, EH, E])
        taps = sb("taps", [P, EH, KW])
        tap_diag = sb("tap_diag", [P, EH, KW, P])
        ident = sb("ident", [P, P])
        pick = sb("pick", [P, N], F32R)
        ones = sb("ones", [P, 1])
        minus_half, eps = sb("minus_half", [P, TJ]), sb("eps", [P, TJ])
        a_coef = sb("a_coef", [P, EH, N])
        inv_a = sb("inv_a", [P, EH, N])
        inv_a_t = sb("inv_a_t", [P, E])
        tiny = sb("tiny", [P, EH, N])
        kept = sb("kept", [P, EH, N])
        d_skip = sb("d_skip", [P, EH])
        flag = sb("flag", [1, 1], I32)
        flag_f = sb("flag_f", [1, 1])

        inv_a_u = hid[:, 0, 0:EH * PROWS].rearrange("p (h n) -> p h n", h=EH)
        flat = ring[:].rearrange("p s n -> p (s n)")
        st_g = flat[:, 0:HM * E]
        st_u = flat[:, HM * E:2 * HM * E]
        st_d = flat[:, 2 * HM * E:3 * HM * E]
        o = 3 * HM * E
        st_z, st_o = flat[:, o:o + EH * E], flat[:, o + EH * E:o + 2 * EH * E]
        o += 2 * EH * E
        st_p, st_dt = flat[:, o:o + E], flat[:, o + E:o + E + EH * R]

        work = [ctx.enter_context(nc.psum_tensor(f"work{i}", [P, CH], F32)) for i in range(BANKS)]
        c_bank = ctx.enter_context(nc.psum_tensor("c_bank", [P, L], F32))

        ready = [sem(f"bank_ready{i}") for i in range(BANKS)]
        free = [sem(f"bank_free{i}") for i in range(BANKS)]
        S = {s: sem(s) for s in K.slope}
        w_landed, w_set, w_turned, w_kept = sem("w_landed"), sem("w_set"), sem("w_turned"), sem("w_kept")
        s_ident, s_exp, s_set, s_flag, s_fix = sem("s_ident"), sem("s_exp"), sem("s_set"), sem("s_flag"), sem("s_fix")

        def wait(eng, what, step, turn, less=0, apart=False):
            if (what, step) not in K.at:
                return
            s, n = K.at[what, step]
            n -= less
            if what in ("ready", "free"):
                s, slope = (ready if what == "ready" else free)[s], K.bank_slope
            else:
                s, slope = S[s], K.slope[s]
            if turn is not None:
                n = eng.to_reg(turn * slope + n) if apart else turn * slope + n
                if apart:
                    eng.wait_ge(s_set, 1)
            eng.wait_ge(s, n)

        def wait_before(eng, what, step, back, turn):
            before = K.prev[what, step]
            if len(before) >= back:
                wait(eng, what, before[-back], turn)

        def bank(job):
            return work[K.bank[job]]

        def done(job):
            return ready[K.bank[job]]

        def freed(job):
            return free[K.bank[job]]

        def parts(eng, part):
            for b in range(-1, LOOP_FROM):
                part(b, None)
            with eng.Fori(0, (LOOP_TO - LOOP_FROM) // 2) as turn:
                for b in (LOOP_FROM, LOOP_FROM + 1):
                    part(b, turn)
            for b in range(LOOP_TO, B + 1):
                part(b, None)

        def row(b, turn):
            return b if turn is None else turn * 2 + b

        weight_loads = 13
        groups = 8 + 3 + 1 + 1 + 1 + 1 + 1

        block = ctx.enter_context(nc.Block())

        @block.sync
        def _(sp):
            for dst, src in (
                (st_g.bitcast(I32).rearrange("p (m e) -> p m e", m=HM), w_gate.rearrange("(m p) e -> p m e", p=P)),
                (st_u.bitcast(I32).rearrange("p (m e) -> p m e", m=HM), w_up.rearrange("(m p) e -> p m e", p=P)),
                (st_d.bitcast(I32).rearrange("p (h k) -> p h k", h=EH), w_down.rearrange("(h p) k -> p h k", p=P)),
                (st_z.rearrange("p (h e) -> p h e", h=EH), W_z.rearrange("(h p) e -> p h e", p=P)),
                (st_o.rearrange("p (h e) -> p h e", h=EH), W_out.rearrange("(h p) e -> p h e", p=P)),
                (st_p[0:R + 2 * N, :], W_params),
                (st_dt.rearrange("p (h r) -> p h r", h=EH), W_dt.rearrange("(h p) r -> p h r", p=P)),
                (a_coef[:], A_log.rearrange("(h p) n -> p h n", p=P)),
                (taps[:], conv_w.rearrange("(h p) o k -> p h (o k)", p=P)),
                (wdt_t[R:R + 1, :], b_dt.rearrange("(o e) -> o e", o=1)),
            ):
                sp.dma_start(dst, src).then_inc(w_landed, 16)
            with nc.allow_non_contiguous_dma(reason="256 numbers, one to a partition"):
                sp.dma_start(d_skip[:], D.rearrange("(h p) -> p h", p=P)).then_inc(w_landed, 16)

            def part(b, turn):
                for ev in steps(b):
                    if ev[0] == "ld":
                        _, bt, c = ev
                        wait(sp, "free", ("dn", 1, bt - 1, c, 1), turn)
                        src = x[row(bt, turn)].rearrange("(c j p) e -> c p j e", c=NC, p=P)[c]
                        sp.dma_start(x_in[:, c * TJ:(c + 1) * TJ, :], src).then_inc(S[f"ld{c}"], 16)
                    elif ev[0] == "st":
                        _, bt, c = ev
                        wait(sp, "free", ("dn", 2, bt, c, 1), turn)
                        dst = out[row(bt, turn)].rearrange("(c j p) e -> c p j e", c=NC, p=P)[c]
                        sp.dma_start(dst, x_fin[:, c * TJ:(c + 1) * TJ, :]).then_inc(S[f"st{c}"], 16)

            parts(sp, part)
            for c in range(NC):
                sp.wait_ge(S[f"st{c}"], 16 * B)

        @block.tensor
        def _(pe):
            pe.wait_ge(s_ident, 2)
            pe.wait_ge(w_set, 3)
            n = 0

            def turn_group(blocks):
                nonlocal n
                if n >= BANKS:
                    pe.wait_ge(w_kept, n - BANKS + 1)
                for i, src in enumerate(blocks):
                    k, m = src.shape
                    last = pe.transpose(work[n % BANKS][0:m, i * P:i * P + k], src, ident[0:k, 0:k])
                last.then_inc(w_turned, 1)
                n += 1

            for w in (st_g, st_u):
                for k in range(EH):
                    for m0 in (0, 4):
                        turn_group([w[:, m * E + k * P:m * E + (k + 1) * P] for m in range(m0, min(m0 + 4, HM))])
            for m0 in range(0, HM, 2):
                turn_group([st_d[:, h * HID + m * P:h * HID + (m + 1) * P] for m in (m0, m0 + 1) for h in range(EH)])
            for w in (st_z, st_o):
                turn_group([w[:, h * E + k * P:h * E + (k + 1) * P] for k in range(EH) for h in range(EH)])
            turn_group([st_p[0:R + 2 * N, k * P:(k + 1) * P] for k in range(EH)])
            turn_group([st_dt[:, h * R:(h + 1) * R] for h in range(EH)])
            pe.wait_ge(s_set, 1)
            turn_group([inv_a_u[:, h, :] for h in range(EH)])
            pe.matmul(c_bank[0:1, 0:EH * N], ones[:], tiny[:].rearrange("p h n -> p (h n)"), start=True,
                      stop=True).then_inc(s_flag, 1)
            pe.wait_ge(w_kept, groups)
            pe.wait_ge(s_flag, 3)

            def part(b, turn):
                def take(job):
                    s, n = K.at["free", job]
                    if n > 1:
                        n -= 1
                        pe.wait_ge(free[s], n if turn is None else turn * K.bank_slope + n)
                    return bank(job)

                for ev in steps(b):
                    kind = ev[0]
                    if kind == "T":
                        wait(pe, "normed", ("lx",) + ev[1:], turn)
                        for h in range(EH):
                            job = ev + (h,)
                            dst = take(job)
                            for j in range(TJ):
                                last = pe.transpose(dst[:, j * P:(j + 1) * P], normed[:, j, h * P:(h + 1) * P], ident[:])
                            last.then_inc(done(job), 1)
                    elif kind == "gu":
                        _, f, bt, c, m = ev
                        wait(pe, "free", ("T", 1 if f == 1 else 3, bt, c, EH - 1), turn)
                        for w, name in ((wg_t, "gate"), (wu_t, "up")):
                            job = ev + (name,)
                            dst = take(job)
                            for k in range(EH):
                                for i, part_ in enumerate((xt_hi[c], xt_lo[c])):
                                    last = pe.matmul(dst[:], w[:, k, m * P:(m + 1) * P], part_[:, k, :],
                                                     start=(k == 0 and i == 0), stop=(k == EH - 1 and i == 1))
                            last.then_inc(done(job), 1)
                    elif kind == "dn":
                        _, f, bt, c, jp = ev
                        wait(pe, "lo", ("lo", f, bt, c, HM - 1), turn)
                        dst = take(ev)
                        for j in range(2):
                            t = (2 * jp + j) * P
                            for m in range(HM):
                                for i, part_ in enumerate((hid_hi, hid_lo)):
                                    last = pe.matmul(dst[:, j * E:(j + 1) * E], part_[:, m, t:t + P], wd_t[:, m, :],
                                                     start=(m == 0 and i == 0), stop=(m == HM - 1 and i == 1))
                        last.then_inc(done(ev), 1)
                    elif kind == "op":
                        _, bt, jp = ev
                        wait(pe, "gated", ("gate", bt), turn)
                        dst = take(ev)
                        for j in range(2):
                            t = (2 * jp + j) * P
                            for h in range(EH):
                                last = pe.matmul(dst[:, j * E:(j + 1) * E], acc[bt % 2][:, h, t:t + P], wo_t[:, h, :],
                                                 start=(h == 0), stop=(h == EH - 1))
                        last.then_inc(done(ev), 1)
                    elif kind == "z":
                        _, bt, h, c = ev
                        dst = take(ev)
                        for k in range(EH):
                            last = pe.matmul(dst[:], wz_t[:, k, h * P:(h + 1) * P],
                                             xt[:, k, KW - 1 + c * CH:KW - 1 + (c + 1) * CH],
                                             start=(k == 0), stop=(k == EH - 1))
                        last.then_inc(done(ev), 1)
                    elif kind == "pm":
                        _, bt, c = ev
                        wait(pe, "free", ("T", 2, bt, c, EH - 2), turn)
                        wait(pe, "free", ("T", 2, bt, c, EH - 1), turn)
                        dst = take(ev)
                        for k in range(EH):
                            last = pe.matmul(dst[0:PROWS, :], wp_t[:, k, :],
                                             xt[:, k, KW - 1 + c * CH:KW - 1 + (c + 1) * CH],
                                             start=(k == 0), stop=(k == EH - 1))
                        last.then_inc(done(ev), 1)
                    elif kind == "cv":
                        _, bt, h, c = ev
                        dst = take(ev)
                        for k in range(KW):
                            last = pe.matmul(dst[:], tap_diag[:, h, k, :], xt[:, h, k + c * CH:k + (c + 1) * CH],
                                             start=(k == 0), stop=(k == KW - 1))
                        last.then_inc(done(ev), 1)
                    elif kind == "dt":
                        _, bt, h, c = ev
                        wait(pe, "c_high", ("pe", bt, c), turn)
                        dst = take(ev)
                        pe.matmul(dst[:], wdt_t[:, h * P:(h + 1) * P], params[0:R + 1, c * CH:(c + 1) * CH],
                                  start=True, stop=True).then_inc(done(ev), 1)
                    elif kind == "rm":
                        _, bt, h, c = ev
                        wait(pe, "c_high", ("pe", bt, c), turn)
                        dst = take(ev)
                        pe.matmul(dst[:], inv_a_t[CD_ROW:CD_ROW + N, h * P:(h + 1) * P],
                                  params[CD_ROW:CD_ROW + N, c * CH:(c + 1) * CH],
                                  start=True, stop=True).then_inc(done(ev), 1)
                    elif kind == "bc":
                        _, bt, s = ev
                        wait(pe, "free", ("pm", bt, NC - 1), turn)
                        if s:
                            wait(pe, "weighted", ("cm", bt, s - 1, EH - 1), turn)
                        else:
                            wait(pe, "weighted", ("cm", bt - 1, N - 1, EH - 1), turn)
                        for c in range(NC):
                            last = pe.matmul(c_bank[:, c * CH:(c + 1) * CH], pick[C_ROW:P, s:s + 1].to_broadcast([P - C_ROW, P]),
                                             c_parts[bt % 2][C_ROW:P, c * CH:(c + 1) * CH], start=True, stop=True)
                        last.then_inc(S["c_spread"], 1)

            parts(pe, part)

        @block.scalar
        def _(act):
            act.wait_ge(w_landed, 16 * 11)
            nc.scalar.activation(a_coef[:], a_coef[:], ACT.Exp).then_inc(s_exp, 1)
            act.wait_ge(w_kept, groups)
            act.wait_ge(s_set, 1)

            def part(b, turn):
                for ev in steps(b):
                    kind = ev[0]
                    if kind == "lx":
                        _, f, bt, c = ev
                        slot = K.at["normed", ev][1] % 2
                        src = {1: x_in, 2: x_mid[bt % 2], 3: x_fin}[f]
                        wait(act, "ready", K.was[ev], turn)
                        wait(act, "rstd", ("lr",) + ev[1:], turn)
                        for j in range(TJ):
                            last = nc.scalar.activation(normed[:, j, :], src[:, c * TJ + j, :], ACT.Identity,
                                                        bias=shift[:, slot, j:j + 1], scale=rstd[:, slot, j:j + 1])
                        last.then_inc(S["normed"], 1)
                    elif kind == "Te":
                        _, f, bt, c = ev
                        for h in range(EH):
                            job = ("T", f, bt, c, h)
                            wait(act, "ready", job, turn)
                            if f == 2:
                                if h == 0:
                                    wait(act, "ready", ("z", bt - 1, EH - 1, NC - 1), turn)
                                nc.scalar.activation(xt[:, h, KW - 1 + c * CH:KW - 1 + (c + 1) * CH], bank(job)[:],
                                                     ACT.Copy).then_inc(freed(job), 1)
                            else:
                                if h == 0:
                                    wait(act, "ready", K.was["T", f, bt, c], turn)
                                nc.scalar.activation(xt_hi[c][:, h, :], bank(job)[:], ACT.Copy, scale=XS).then_inc(S["xhi"], 1)
                    elif kind == "th":
                        job = ev[1:] + (("gate",) if ev[1] == "gu" else ())
                        wait(act, "ready", job, turn)
                        before = K.prev["tanh", ev]
                        if len(before) == TANHS:
                            was = before[0][1:]
                            wait(act, "free", was + ("gate",) if was[0] == "gu" else was, turn)
                        slot = K.at["tanh", ev][1] % TANHS
                        nc.scalar.activation(tanh[:, slot, :], bank(job)[:], ACT.Tanh,
                                             scale=GATE_HALF if ev[1] == "gu" else 0.5).then_inc(S["tanh"], 1)
                    elif kind == "hi":
                        _, f, bt, c, m = ev
                        wait(act, "free", ("gu",) + ev[1:] + ("up",), turn)
                        if m == 0:
                            wait(act, "ready", K.was[ev], turn)
                        slot = K.at["hi", ev][1] % HIDS
                        nc.scalar.activation(hid_hi[:, m, :], hid[:, slot, :], ACT.Copy).then_inc(S["hi"], 1)
                    elif kind == "pe":
                        _, bt, c = ev
                        job = ("pm", bt, c)
                        wait(act, "ready", job, turn)
                        wait(act, "ready", ("rm", bt - 1, EH - 1, c), turn)
                        wait(act, "c_spread", ("bc", bt - 2, N - 1), turn)
                        src, t = bank(job), slice(c * CH, (c + 1) * CH)
                        nc.scalar.activation(params[0:R, t], src[0:R, :], ACT.Copy)
                        nc.scalar.activation(params[CD_ROW:CD_ROW + N, t], src[CD_ROW:CD_ROW + N, :], ACT.Copy)
                        nc.scalar.activation(c_parts[bt % 2][C_ROW:C_ROW + N, t], src[C_ROW:C_ROW + N, :], ACT.Copy)
                        nc.scalar.activation(c_parts[bt % 2][CD_ROW:CD_ROW + N, t], src[CD_ROW:CD_ROW + N, :],
                                             ACT.Copy).then_inc(S["c_high"], 1)
                    elif kind == "da":
                        _, bt, h, c = ev
                        job = ("dt",) + ev[1:]
                        wait(act, "ready", job, turn)
                        wait(act, "scanned", ("scan", bt - 2, N - 1, EH - 1), turn)
                        y = dt[bt % 2][:, h, 1 + c * CH:1 + (c + 1) * CH]
                        nc.scalar.activation(y, bank(job)[:], ACT.Abs).then_inc(S["sp_exp"], 1)
                        wait(act, "sp_added", ("df", bt, h - 1, c) if h else ("df", bt - 1, EH - 1, c), turn)
                        nc.scalar.activation(sp_r[:, c, :], bank(job)[:], ACT.Relu).then_inc(freed(job), 1)
                        wait(act, "sp_exp", ev, turn, less=1)
                        nc.scalar.activation(y, y, ACT.Exp, scale=-1.0).then_inc(S["sp_exp"], 1)
                    elif kind == "dl":
                        _, bt, h, c = ev
                        wait(act, "sp_exp", ("da", bt, h, c), turn)
                        wait(act, "sp_sum", ("dp", bt, h - 1, c) if h else ("dp", bt - 1, EH - 1, c), turn)
                        nc.scalar.activation(sp_l[:, c, :], dt[bt % 2][:, h, 1 + c * CH:1 + (c + 1) * CH], ACT.Ln,
                                             bias=1.0).then_inc(S["sp_ln"], 1)
                    elif kind == "ex":
                        _, bt, s, h = ev
                        if s == 0 and h == 0:
                            wait(act, "dt_first", ("dt0", bt), turn)
                        before = K.prev["decay", ev]
                        if len(before) >= DECAYS:
                            wait(act, "scanned", ("scan",) + before[-DECAYS][1:], turn)
                        slot = K.at["decay", ev][1] % DECAYS
                        nc.scalar.activation(decay[:, slot, :], dt[bt % 2][:, h, 0:L], ACT.Exp,
                                             scale=a_coef[:, h, s:s + 1]).then_inc(S["decay"], 1)

            parts(act, part)

        @block.gpsimd
        def _(pool):
            nc.gpsimd.memset(ident[:], 0.0).then_inc(s_ident, 1)
            pool.wait_ge(s_ident, 1)
            nc.gpsimd.affine_select(out=ident[:], in_=ident[:], compare_op=ALU.not_equal, fill=1.0, base=0,
                                    pattern=[[-1, P]], channel_multiplier=1).then_inc(s_ident, 1)
            pool.wait_ge(w_kept, groups)
            pool.wait_ge(s_set, 1)
            def part(b, turn):
                for ev in steps(b):
                    kind = ev[0]
                    if kind == "lr":
                        _, f, bt, c = ev
                        slot = K.at["rstd", ev][1] // 4 % 2
                        r = rstd[:, slot, :]
                        before = K.prev["rstd", ev]
                        if len(before) >= 2:
                            wait(pool, "normed", ("lx",) + before[-2][1:], turn)
                        wait(pool, "meanvar", ("ln",) + ev[1:], turn)
                        nc.gpsimd.tensor_tensor(r, meanvar[:, slot, :, 1], eps[:], ALU.add).then_inc(S["rstd"], 1)
                        wait(pool, "rstd", ev, turn, less=3)
                        nc.gpsimd.tensor_tensor(r, r, minus_half[:], ALU.pow).then_inc(S["rstd"], 1)
                        wait(pool, "rstd", ev, turn, less=2)
                        nc.gpsimd.tensor_tensor(shift[:, slot, :], meanvar[:, slot, :, 0], r, ALU.mult).then_inc(S["rstd"], 1)
                        wait(pool, "rstd", ev, turn, less=1, apart=True)
                        nc.gpsimd.tensor_scalar(shift[:, slot, :], shift[:, slot, :], -1.0, None, ALU.mult).then_inc(S["rstd"], 1)
                    elif kind == "lo":
                        m = ev[4]
                        wait(pool, "hi", ("hi",) + ev[1:], turn)
                        slot = K.at["lo", ev][1] % HIDS
                        nc.gpsimd.tensor_tensor(hid_lo[:, m, :], hid[:, slot, :], hid_hi[:, m, :],
                                                ALU.subtract).then_inc(S["lo"], 1)
                    elif kind == "dp":
                        _, bt, h, c = ev
                        y = dt[bt % 2][:, h, 1 + c * CH:1 + (c + 1) * CH]
                        wait_before(pool, "sp_sum", ev, 1, turn)
                        wait(pool, "sp_ln", ("dl", bt, h, c), turn, apart=True)
                        nc.gpsimd.tensor_scalar(sp_v[:], y, 1.0, 1.0, ALU.add, ALU.subtract).then_inc(S["sp_sum"], 1)
                        wait(pool, "sp_sum", ev, turn, less=2)
                        nc.gpsimd.tensor_tensor(sp_l[:, c, :], sp_l[:, c, :], sp_v[:], ALU.subtract).then_inc(S["sp_sum"], 1)
                        wait(pool, "sp_sum", ev, turn, less=1)
                        nc.gpsimd.tensor_tensor(y, sp_l[:, c, :], y, ALU.add).then_inc(S["sp_sum"], 1)
                    elif kind == "cm":
                        _, bt, s, h = ev
                        if s == 0 and h == 0:
                            wait(pool, "acc_begun", ("ai", bt, EH - 1, NC - 1), turn)
                        wait(pool, "weighted", ev, turn)
                        wait_before(pool, "summed", ev, 2, turn)
                        slot = K.at["weighted", ev][1] % 2
                        nc.gpsimd.tensor_tensor(acc[bt % 2][:, h, :], acc[bt % 2][:, h, :], cg[:, slot, :],
                                                ALU.add).then_inc(S["summed"], 1)
                    elif kind == "d":
                        _, bt, h = ev
                        if h == 0:
                            wait(pool, "u_first", ("u0", bt), turn)
                        wait(pool, "scanned", ("scan", bt - 1, N - 1, h), turn)
                        nc.gpsimd.tensor_tensor(du[:, h, :], u[bt % 2][:, h, 1:1 + L], u[bt % 2][:, h, 0:L],
                                                ALU.subtract).then_inc(S["du"], 1)

            parts(pool, part)

        @block.vector
        def _(dve):
            own = 0

            def then(ins):
                nonlocal own
                own += 1
                ins.then_inc(w_set, 1)
                dve.wait_ge(w_set, own)

            dve.wait_ge(w_landed, 16 * 11)
            for w in (st_g, st_u, st_d):
                then(nc.vector.tensor_copy(w, w.bitcast(I32)))
            for t in (wp_t[:], inv_a_u, pick[:].bitcast(F32), c_parts[0][:].bitcast(F32), c_parts[1][:].bitcast(F32),
                      xt[:, :, 0:KW - 1], u[0][:, :, 0:1], u[1][:, :, 0:1], params[C_ROW:P, :]):
                then(nc.vector.memset(t, 0.0))
            then(nc.vector.memset(ones[:], 1.0))
            then(nc.vector.memset(minus_half[:], -0.5))
            then(nc.vector.memset(eps[:], EPS))
            then(nc.vector.memset(params[R:R + 1, :], 1.0))
            dve.wait_ge(s_ident, 2)
            then(nc.vector.tensor_copy(pick[C_ROW:C_ROW + N, :], ident[C_ROW:C_ROW + N, C_ROW:C_ROW + N]))
            then(nc.vector.tensor_copy(pick[CD_ROW:CD_ROW + N, :], ident[CD_ROW:CD_ROW + N, CD_ROW:CD_ROW + N]))
            for h in range(EH):
                for k in range(KW):
                    then(nc.vector.tensor_scalar(tap_diag[:, h, k, :], ident[:], taps[:, h, k:k + 1], None, ALU.mult))
            dve.wait_ge(s_exp, 1)
            then(nc.vector.tensor_scalar(tiny[:], a_coef[:], A_MIN, None, ALU.is_lt))
            then(nc.vector.tensor_scalar(a_coef[:], a_coef[:], -1.0, None, ALU.mult))
            then(nc.vector.tensor_scalar(kept[:], tiny[:], -1.0, 1.0, ALU.mult, ALU.add))
            then(nc.vector.scalar_tensor_tensor(inv_a[:], a_coef[:], 1e-10, kept[:], ALU.add, ALU.mult))
            then(nc.vector.tensor_tensor(inv_a[:], inv_a[:], tiny[:], ALU.subtract))
            then(nc.vector.reciprocal(inv_a[:], inv_a[:]))
            then(nc.vector.tensor_tensor(inv_a[:], inv_a[:], kept[:], ALU.mult))
            then(nc.vector.tensor_copy(inv_a_u[:, :, CD_ROW:CD_ROW + N], inv_a[:]))
            then(nc.vector.tensor_tensor(inv_a[:], inv_a[:], tiny[:], ALU.add))
            nc.vector.tensor_copy(flag_f[:], ones[0:1, :]).then_inc(s_set, 1)
            n = 0

            def keep(copies):
                nonlocal n
                dve.wait_ge(w_turned, n + 1)
                for dst, src in copies(work[n % BANKS]):
                    last = nc.vector.tensor_copy(dst, src)
                last.then_inc(w_kept, 1)
                n += 1

            for w in (wg_t, wu_t):
                for k in range(EH):
                    for m0, m1 in ((0, 4), (4, HM)):
                        keep(lambda ps: [(w[:, k, m0 * P:m1 * P], ps[:, 0:(m1 - m0) * P])])
            for m0 in range(0, HM, 2):
                keep(lambda ps: [(wd_t[:, m0:m0 + 2, :].rearrange("p m e -> p (m e)"), ps[:])])
            for w in (wz_t, wo_t):
                keep(lambda ps: [(w[:].rearrange("p k e -> p (k e)"), ps[:])])
            keep(lambda ps: [(wp_t[:, k, a:a + m], ps[:, k * P + o:k * P + o + m]) for k in range(EH)
                             for a, o, m in ((0, 0, R), (C_ROW, R + N, N), (CD_ROW, R + N, N))])
            keep(lambda ps: [(wdt_t[0:R, :], ps[0:R, 0:E])])
            keep(lambda ps: [(inv_a_t[CD_ROW:CD_ROW + N, :], ps[CD_ROW:CD_ROW + N, 0:E])])
            dve.wait_ge(s_flag, 1)
            nc.vector.tensor_reduce(flag_f[:], c_bank[0:1, 0:EH * N], AX_X, ALU.add).then_inc(s_flag, 1)
            dve.wait_ge(s_flag, 2)
            nc.vector.tensor_copy(flag[:], flag_f[:]).then_inc(s_flag, 1)
            dve.wait_ge(s_flag, 3)
            dve.wait_ge(w_kept, groups)
            n_tiny = dve.value_load(flag[0:1, 0:1])

            def program(with_tiny):
                def part(b, turn):
                    for ev in steps(b):
                        kind = ev[0]
                        if kind == "ln":
                            _, f, bt, c = ev
                            slot = K.at["meanvar", ev][1] % 2
                            src = {1: x_in, 2: x_mid[bt % 2], 3: x_fin}[f]
                            if f == 1:
                                wait(dve, f"ld{c}", ("ld", bt, c), turn)
                            elif f == 2:
                                wait(dve, "free", ("dn", 1, bt, c, 1), turn)
                            else:
                                wait(dve, "free", ("op", bt, 2 * c + 1), turn)
                            before = K.prev["meanvar", ev]
                            if len(before) >= 2:
                                wait(dve, "normed", ("lx",) + before[-2][1:], turn)
                            for j in range(TJ):
                                last = nc.vector.bn_stats(stats[:, slot, j, :], src[:, c * TJ + j, :])
                            last.then_inc(S["stats"], 1)
                            wait(dve, "stats", ev, turn, apart=True)
                            for j in range(TJ):
                                last = nc.vector.bn_aggr(meanvar[:, slot, j, :], stats[:, slot, j, :])
                            last.then_inc(S["meanvar"], 1)
                        elif kind == "Tl":
                            _, f, bt, c = ev
                            for h in range(EH):
                                job = ("T",) + ev[1:] + (h,)
                                if h == 0:
                                    wait(dve, "xhi", ("Te",) + ev[1:], turn)
                                nc.vector.scalar_tensor_tensor(xt_lo[c][:, h, :], bank(job)[:], XS, xt_hi[c][:, h, :],
                                                               ALU.mult, ALU.subtract).then_inc(freed(job), 1)
                        elif kind == "sh":
                            gu = ("gu",) + ev[1:]
                            wait(dve, "tanh", ("th",) + gu, turn)
                            i = K.at["lo", ("lo",) + ev[1:]][1] % HIDS
                            wait_before(dve, "lo", ("lo",) + ev[1:], HIDS, turn)
                            nc.vector.scalar_tensor_tensor(hid[:, i, :], tanh[:, K.at["tanh", ("th",) + gu][1] % TANHS, :], 1.0,
                                                           bank(gu + ("gate",))[:], ALU.add,
                                                           ALU.mult).then_inc(freed(gu + ("gate",)), 1)
                            wait(dve, "free", gu + ("gate",), turn)
                            wait(dve, "ready", gu + ("up",), turn)
                            nc.vector.scalar_tensor_tensor(hid[:, i, :], hid[:, i, :], H_SCALE, bank(gu + ("up",))[:],
                                                           ALU.mult, ALU.mult).then_inc(freed(gu + ("up",)), 1)
                        elif kind == "rs":
                            _, f, bt, c, jp = ev
                            job = ("dn",) + ev[1:]
                            t = slice(c * TJ + 2 * jp, c * TJ + 2 * jp + 2)
                            src, dst = (x_in, x_mid[bt % 2]) if f == 1 else (x_fin, x_fin)
                            wait(dve, "ready", job, turn)
                            nc.vector.scalar_tensor_tensor(
                                dst[:, t, :].rearrange("p j e -> p (j e)"), bank(job)[:], OUT_SCALE,
                                src[:, t, :].rearrange("p j e -> p (j e)"), ALU.mult, ALU.add).then_inc(freed(job), 1)
                        elif kind == "ra":
                            _, bt, jp = ev
                            job = ("op", bt, jp)
                            t = slice(2 * jp, 2 * jp + 2)
                            wait(dve, f"st{jp // 2}", ("st", bt - 1, jp // 2), turn)
                            wait(dve, "ready", job, turn)
                            nc.vector.tensor_tensor(
                                x_fin[:, t, :].rearrange("p j e -> p (j e)"), bank(job)[:],
                                x_mid[bt % 2][:, t, :].rearrange("p j e -> p (j e)"), ALU.add).then_inc(freed(job), 1)
                        elif kind == "gate":
                            _, bt = ev
                            wait(dve, "summed", ("cm", bt, N - 1, EH - 1), turn)
                            for h in range(EH):
                                nc.vector.scalar_tensor_tensor(acc[bt % 2][:, h, :], acc[bt % 2][:, h, :], 0.25, zs[:, h, :],
                                                               ALU.mult, ALU.mult).then_inc(S["gated"], 1)
                        elif kind == "zs":
                            _, bt, h, c = ev
                            job = ("z",) + ev[1:]
                            wait(dve, "tanh", ("th",) + job, turn)
                            wait(dve, "gated", ("gate", bt - 1), turn)
                            nc.vector.scalar_tensor_tensor(zs[:, h, c * CH:(c + 1) * CH], tanh[:, K.at["tanh", ("th",) + job][1] % TANHS, :], 1.0,
                                                           bank(job)[:], ALU.add, ALU.mult).then_inc(freed(job), 1)
                        elif kind == "pl":
                            _, bt = ev
                            for c in range(NC):
                                job = ("pm", bt, c)
                                wait(dve, "c_high", ("pe", bt, c), turn)
                                low = c_parts[bt % 2][CD_ROW:CD_ROW + N, c * CH:(c + 1) * CH]
                                nc.vector.tensor_tensor(low, bank(job)[CD_ROW:CD_ROW + N, :], low.bitcast(F32),
                                                        ALU.subtract).then_inc(freed(job), 1)
                        elif kind == "us":
                            _, bt, h, c = ev
                            job = ("cv",) + ev[1:]
                            wait(dve, "tanh", ("th",) + job, turn)
                            wait(dve, "du", ("d", bt - 2, EH - 1), turn)
                            nc.vector.scalar_tensor_tensor(u[bt % 2][:, h, 2 + c * CH:2 + (c + 1) * CH],
                                                           tanh[:, K.at["tanh", ("th",) + job][1] % TANHS, :], 1.0, bank(job)[:],
                                                           ALU.add, ALU.mult).then_inc(freed(job), 1)
                        elif kind == "u0":
                            _, bt = ev
                            wait(dve, "free", ("cv", bt, EH - 1, 0), turn)
                            nc.vector.tensor_copy(u[bt % 2][:, :, 1:2], u[bt % 2][:, :, 2:3]).then_inc(S["u_first"], 1)
                        elif kind == "df":
                            _, bt, h, c = ev
                            y = dt[bt % 2][:, h, 1 + c * CH:1 + (c + 1) * CH]
                            wait(dve, "free", ("dt",) + ev[1:], turn)
                            wait(dve, "sp_sum", ("dp",) + ev[1:], turn)
                            nc.vector.tensor_tensor(y, sp_r[:, c, :], y, ALU.add).then_inc(S["sp_added"], 1)
                        elif kind == "dt0":
                            _, bt = ev
                            for h in range(EH):
                                wait(dve, "sp_added", ("df", bt, h, 0), turn)
                            nc.vector.tensor_copy(dt[bt % 2][:, :, 0:1], dt[bt % 2][:, :, 1:2]).then_inc(S["dt_first"], 1)
                        elif kind == "ai":
                            _, bt, h, c = ev
                            job = ("rm",) + ev[1:]
                            t = acc[bt % 2][:, h, c * CH:(c + 1) * CH]
                            wait(dve, "ready", job, turn)
                            wait(dve, "u_first", ("u0", bt), turn)
                            nc.vector.tensor_tensor(t, bank(job)[:], u[bt % 2][:, h, 1 + c * CH:1 + (c + 1) * CH],
                                                    ALU.mult).then_inc(freed(job), 1)
                            wait(dve, "free", job, turn)
                            nc.vector.scalar_tensor_tensor(t, u[bt % 2][:, h, 2 + c * CH:2 + (c + 1) * CH], d_skip[:, h:h + 1], t,
                                                           ALU.mult, ALU.subtract).then_inc(S["acc_begun"], 1)
                        elif kind == "scan":
                            _, bt, s, h = ev
                            i, a = K.at["scanned", ev][1] % 2, K.at["decay", ("ex",) + ev[1:]][1] % DECAYS
                            if s == 0:
                                wait(dve, "du", ("d", bt, h), turn)
                            wait(dve, "decay", ("ex",) + ev[1:], turn)
                            was = K.prev["scanned", ev][-2:]
                            if len(was) == 2:
                                wait(dve, "weighted", ("cm",) + was[0][1:], turn)
                            scan = nc.vector.tensor_tensor_scan(g[:, i, :], du[:, h, :], decay[:, a, :], 0.0, ALU.add, ALU.mult)
                            if not with_tiny:
                                scan.then_inc(S["scanned"], 1)
                                continue
                            _, k = K.at["scanned", ev]
                            at = 4 * (k - 1) if turn is None else turn * (4 * K.slope["scanned"]) + 4 * (k - 1)
                            scan.then_inc(s_fix, 1)
                            if len(was) == 2:
                                wait(dve, "summed", ("cm",) + was[0][1:], turn)
                            v = cg[:, i, :]
                            nc.vector.scalar_tensor_tensor(v, dt[bt % 2][:, h, 0:L], tiny[:, h, s:s + 1], u[bt % 2][:, h, 1:1 + L],
                                                           ALU.mult, ALU.mult).then_inc(s_fix, 1)
                            dve.wait_ge(s_fix, at + 2)
                            nc.vector.tensor_tensor_scan(v, decay[:, a, :], v, 0.0, ALU.mult, ALU.add).then_inc(s_fix, 1)
                            dve.wait_ge(s_fix, at + 3)
                            nc.vector.tensor_scalar(g[:, i, :], g[:, i, :], kept[:, h, s:s + 1], None, ALU.mult).then_inc(s_fix, 1)
                            dve.wait_ge(s_fix, at + 4)
                            nc.vector.tensor_tensor(g[:, i, :], g[:, i, :], v, ALU.add).then_inc(S["scanned"], 1)
                        elif kind == "cm":
                            _, bt, s, h = ev
                            i = K.at["weighted", ev][1] % 2
                            wait(dve, "scanned", ("scan",) + ev[1:], turn)
                            wait(dve, "c_spread", ("bc", bt, s), turn)
                            was = K.prev["weighted", ev][-2:]
                            if len(was) == 2:
                                wait(dve, "summed", was[0], turn)
                            nc.vector.scalar_tensor_tensor(cg[:, i, :], g[:, i, :], inv_a[:, h, s:s + 1], c_bank[:],
                                                           ALU.mult, ALU.mult).then_inc(S["weighted"], 1)

                parts(dve, part)

            with dve.If(n_tiny > 0):
                program(True)
            with dve.Else():
                program(False)


INS = ("L0_attn_x", "L0_attn_W_z", "L0_attn_W_params", "L0_attn_conv_w", "L0_attn_W_dt", "L0_attn_b_dt", "L0_attn_A_log",
       "L0_attn_D", "L0_attn_W_out", "L0_ffn_w_gate", "L0_ffn_w_up", "L0_ffn_w_down")


def kernel(**inputs):
    import concourse.bacc as bacc
    from concourse.bass_utils import run_bass_kernel_spmd

    nc = bacc.Bacc("TRN2", target_bir_lowering=False, num_devices=1, dynamic_dma_scratch_size=1024)
    arrays, args = {}, []
    for name in INS:
        a = np.ascontiguousarray(inputs[name])
        arrays[name] = a
        args.append(nc.dram_tensor(name, a.shape, mybir.dt.from_np(a.dtype), kind="ExternalInput").ap())
    out = nc.dram_tensor("out", (B, L, E), F32, kind="ExternalOutput").ap()
    macaron_kernel(nc, *args, out)
    return run_bass_kernel_spmd(nc, [arrays], core_ids=[0]).results[0]["out"]
```

```python
from contextlib import ExitStack

import numpy as np

import concourse.bass as bass
from concourse import mybir

ALU = mybir.AluOpType
ACT = mybir.ActivationFunctionType
AX_X = mybir.AxisListType.X
F32 = mybir.dt.float32
F32R = mybir.dt.float32r
F16 = mybir.dt.float16
I32 = mybir.dt.int32

P = 128
B, L, E = 16, 1024, 256
HID = 768
N, KW, R = 16, 4, 64
EH = E // P
CH = 512
NC = L // CH
TJ = CH // P
HM = HID // P
AHEAD, DECAYS = 2, 4
TERMS = 2
HIDS = 3
TANHS = 4
BANKS = 6
EPS = 1e-5
A_MIN = 1e-5
XS = 1024.0
Q = 127.0
GATE_HALF = 0.5 / (XS * Q)
H_SCALE = 0.25 / (XS * Q) ** 2
OUT_SCALE = 1.0 / Q
C_ROW, CD_ROW = 64, 96
PROWS = CD_ROW + N
LOOP_FROM, LOOP_TO = 2, 14


AT = {
    "gate": [0.87], "op": [3.88, 3.99, 4.08, 4.42], "ra": [3.44, 4.99, 5.66, 6.46], "dn1": [8.69, 8.72, 15.44, 15.85],
    "rs1": [8.8, 8.9, 16.04, 16.05], "dn2": [22.12, 22.8, 29.25, 31.79], "rs2": [22.88, 23.43, 32.25, 33.28],
    "ln3": [5.25, 9.94], "lr3": [5.75, 9.69], "lx3": [8.74, 12.06], "T3": [9.26, 14.82], "Te3": [9.38, 14.95],
    "Ts3": [11.21, 14.82], "Tl3": [11.26, 15.37], "ln2": [9.7, 16.14], "lr2": [9.64, 15.45], "lx2": [11.19, 17.3],
    "T2": [11.62, 17.93], "Te2": [14.99, 18.7], "ln1": [20.5, 27.62], "lr1": [20.62, 29.25], "lx1": [23.62, 32],
    "T1": [30, 33.76], "Te1": [28.38, 33.37], "Ts1": [30.2, 36.33], "Tl1": [29.38, 42.76], "pm": [18.57, 19.3],
    "pe": [19.2, 19.49], "pl": [20.37], "cv": [19.75, 21.88, 25.25, 26.62], "thcv": [20.44, 22.13, 25.18, 26.25],
    "us": [21.74, 22.69, 26.36, 27.07], "u0": [28.38], "dt": [20.75, 20.12, 24.07, 25.57], "da": [21.5, 20.5, 25.2, 26.07],
    "dl": [22.62, 22.88, 27.57, 27.57], "dp": [22.68, 23.62, 27.64, 28.95], "dt0": [31.18],
    "rm": [26.38, 27.89, 28.38, 30.38], "ai": [29.38, 28.45, 29.75, 34.84], "z": [4.56, 5.69, 4.56, 6.44],
    "thz": [5.68, 5.06, 4.31, 5.68], "zs": [6.56, 6.8, 5.56, 6.68], "gu1": [-2, 7], "gu2": [14, 21], "st": [30, 33.37],
    "ld": [12.51, 14.25], "d": [36.49, 38.99],
    "bc": [-0.1, 0.9, 1.15, 0.9, 1.15, 0.9, 0.9, 0.9, 1.02, 0.9, 0.9, 0.9, 1.52, 0.9, 0.9, 0.9], "cm": [1.4], "ex": [0.02],
}
PACE = {"gu1": 0.9, "gu2": 0.95}
LAGS = {"th": 0.23, "sh": 0.93, "hi": 1.94, "lo": 2.21}


def steps(b):
    ssm, ffn1, ffn2, ln1 = 0 <= b < B, 0 <= b + 1 < B, 0 <= b - 1 < B, 1 <= b + 2 < B
    out = []

    def put(name, i, *ev):
        out.append((AT[name][i], len(out), ev))

    def rows(f, bt):
        for c in range(NC):
            for kind in ("ln", "lr", "lx", "T", "Te") + (("Ts", "Tl") if f != 2 else ()):
                put(f"{kind}{f}", c, kind, f, bt, c)

    def hidden(f, bt):
        for c in range(NC):
            for m in range(HM):
                q = AT[f"gu{f}"][c] + m * PACE[f"gu{f}"]
                for lag, ev in ((0, ("gu",)), (LAGS["th"], ("th", "gu")), (LAGS["sh"], ("sh",)), (LAGS["hi"], ("hi",)),
                                (LAGS["lo"], ("lo",))):
                    out.append((q + lag, len(out), ev + (f, bt, c, m)))

    def down(f, bt):
        for c in range(NC):
            for jp in range(2):
                put(f"dn{f}", 2 * c + jp, "dn", f, bt, c, jp)
                put(f"rs{f}", 2 * c + jp, "rs", f, bt, c, jp)

    if ssm:
        for q in range(2 * N):
            out.append((q, -1, ("scan", b, q // EH, q % EH)))
            out.append((q + AT["cm"][0], len(out), ("cm", b, q // EH, q % EH)))
        for s in range(N):
            out.append((EH * s + AT["bc"][s], len(out), ("bc", b, s)))
        for h in range(EH):
            for c in range(NC):
                put("z", EH * h + c, "z", b, h, c)
                put("thz", EH * h + c, "th", "z", b, h, c)
                put("zs", EH * h + c, "zs", b, h, c)
    for q in range(2 * N):
        row, slot = (b, q + AHEAD) if q + AHEAD < 2 * N else (b + 1, q + AHEAD - 2 * N)
        if 0 <= row < B:
            out.append((q + AT["ex"][0], len(out), ("ex", row, slot // EH, slot % EH)))
    if ffn2:
        put("gate", 0, "gate", b - 1)
        for jp in range(2 * NC):
            put("op", jp, "op", b - 1, jp)
            put("ra", jp, "ra", b - 1, jp)
        rows(3, b - 1)
        hidden(2, b - 1)
        down(2, b - 1)
        for c in range(NC):
            put("st", c, "st", b - 1, c)
    if ffn1:
        hidden(1, b + 1)
        down(1, b + 1)
        rows(2, b + 1)
        for c in range(NC):
            put("pm", c, "pm", b + 1, c)
            put("pe", c, "pe", b + 1, c)
        put("pl", 0, "pl", b + 1)
        for h in range(EH):
            for c in range(NC):
                i = EH * h + c
                put("cv", i, "cv", b + 1, h, c)
                put("thcv", i, "th", "cv", b + 1, h, c)
                put("us", i, "us", b + 1, h, c)
                for kind in ("dt", "da", "dl", "dp", "rm", "ai"):
                    put(kind, i, kind, b + 1, h, c)
            put("d", h, "d", b + 1, h)
        put("u0", 0, "u0", b + 1)
        put("dt0", 0, "dt0", b + 1)
    if ln1:
        for c in range(NC):
            put("ld", c, "ld", b + 2, c)
        rows(1, b + 2)
    first = []
    if b == -1:
        for c in range(NC):
            first += [("ld", 0, c)] + [(k, 1, 0, c) for k in ("ln", "lr", "lx", "T", "Te", "Ts", "Tl")]
    return first + [ev for _, _, ev in sorted(out)]


class Counts:

    def __init__(self):
        self.at, self.bank, self.prev, self.total, self.was = {}, {}, {}, {}, {}
        last = {}
        self.slope = {}
        count, jobs, order = {}, 0, {}
        for b in range(-1, B + 1):
            for ev in steps(b):
                kind = ev[0]
                if kind == "T" and ev[1] != 2:
                    self.was[ev] = last.get(("gu", ev[3]))
                elif kind == "hi":
                    self.was[ev] = last.get("dn")
                elif kind == "lx":
                    self.was[ev] = last.get("T")
                if kind in ("lx", "T"):
                    assert last.get("row", "T") != kind, "rows are normalised and transposed in turns"
                    last["row"] = kind
                if kind == "gu":
                    last["gu", ev[3]] = ev + ("up",)
                elif kind == "dn":
                    last["dn"] = ev
                elif kind == "T":
                    last["T"] = ev + (EH - 1,)
                for job in self.jobs(ev):
                    k = jobs % BANKS
                    self.bank[job] = k
                    self.at["ready", job] = self.at["free", job] = (k, jobs // BANKS + 1)
                    jobs += 1
                for sem, n in self.increments(ev):
                    for i in range(n):
                        count[sem] = count.get(sem, 0) + 1
                    self.at[sem, ev] = (sem, count[sem])
                    before = order.setdefault(sem, [])
                    self.prev[sem, ev] = list(before[-TANHS:])
                    before.append(ev)
            self.total[b] = dict(count, jobs=jobs)
        one, two = self.total[LOOP_FROM - 1], self.total[LOOP_FROM + 1]
        self.slope = {s: two[s] - one[s] for s in two if s != "jobs"}
        assert (two["jobs"] - one["jobs"]) % BANKS == 0
        self.bank_slope = (two["jobs"] - one["jobs"]) // BANKS

    @staticmethod
    def jobs(ev):
        kind = ev[0]
        if kind == "gu":
            return [ev + ("gate",), ev + ("up",)]
        if kind == "T":
            return [ev + (h,) for h in range(EH)]
        return [ev] if kind in ("dn", "op", "z", "pm", "cv", "dt", "rm") else []

    @staticmethod
    def increments(ev):
        kind = ev[0]
        if kind == "ln":
            return [("stats", 1), ("meanvar", 1)]
        if kind == "Te":
            return [("xhi", EH)] if ev[1] != 2 else []
        if kind == "cm":
            return [("weighted", 1), ("summed", 1)]
        one = {"bc": "c_spread", "gate": "gated", "pe": "c_high", "u0": "u_first", "dt0": "dt_first", "ai": "acc_begun",
               "d": "du", "da": "sp_exp", "dl": "sp_ln", "dp": "sp_sum", "th": "tanh", "hi": "hi",
               "lo": "lo", "lr": "rstd", "Ts": "lowered", "lx": "normed", "ex": "decay", "scan": "scanned"}
        if kind in one:
            return [(one[kind], {"gate": EH, "da": 2, "dp": 3, "dl": 3, "lr": 4, "Ts": EH}.get(kind, 1))]
        if kind in ("ld", "st"):
            return [(f"{kind}{ev[2]}", 16)]
        return []


def macaron_kernel(nc, x, W_z, W_params, conv_w, W_dt, b_dt, A_log, D, W_out, w_gate, w_up, w_down, out):
    K = Counts()

    with ExitStack() as ctx:
        def sb(name, shape, dt=F32):
            return ctx.enter_context(nc.sbuf_tensor(name, shape, dt))

        def sem(name):
            return ctx.enter_context(nc.semaphore(name))

        x_in = sb("x_in", [P, NC * TJ, E])
        x_mid = [sb(f"x_mid{i}", [P, NC * TJ, E]) for i in range(2)]
        x_fin = sb("x_fin", [P, NC * TJ, E])
        normed = sb("normed", [P, TJ, E])
        stats = sb("stats", [P, 2, TJ, 6])
        meanvar = sb("meanvar", [P, 2, TJ, 2])
        rstd = sb("rstd", [P, 2, TJ])
        shift = sb("shift", [P, 2, TJ])
        xt_hi = [sb(f"xt_hi{i}", [P, EH, CH], F16) for i in range(2)]
        xt_lo = [sb(f"xt_lo{i}", [P, EH, CH], F16) for i in range(2)]
        xt = sb("xt", [P, EH, KW - 1 + L])
        tanh = sb("tanh", [P, TANHS, CH])
        hid = sb("hid", [P, HIDS, CH])
        hid_hi = sb("hid_hi", [P, HM, CH], F16)
        hid_lo = sb("hid_lo", [P, HM, CH], F16)
        zs = sb("zs", [P, EH, L])
        u = [sb(f"u{i}", [P, EH, 2 + L]) for i in range(2)]
        du = sb("du", [P, EH, L])
        dt = [sb(f"dt{i}", [P, EH, 1 + L]) for i in range(2)]
        params = sb("params", [P, L])
        c_parts = [sb(f"c_parts{i}", [P, L], F32R) for i in range(2)]
        ring = sb("ring", [P, DECAYS + 2 + TERMS, L])
        decay, g, cg = ring[:, 0:DECAYS, :], ring[:, DECAYS:DECAYS + 2, :], ring[:, DECAYS + 2:DECAYS + 2 + TERMS, :]
        acc = [sb(f"acc{i}", [P, EH, L]) for i in range(2)]
        sp_l = sb("sp_l", [P, 2, CH])
        sp_r = sb("sp_r", [P, 2, CH])
        sp_v = sb("sp_v", [P, 2, CH])
        wg_t = sb("wg_t", [P, EH, HID], F16)
        wu_t = sb("wu_t", [P, EH, HID], F16)
        wd_t = sb("wd_t", [P, HM, E], F16)
        wz_t = sb("wz_t", [P, EH, E])
        wp_t = sb("wp_t", [P, EH, PROWS])
        wdt_t = sb("wdt_t", [R + 1, E])
        wo_t = sb("wo_t", [P, EH, E])
        taps = sb("taps", [P, EH, KW])
        tap_diag = sb("tap_diag", [P, EH, KW, P])
        ident = sb("ident", [P, P])
        neg_ident = sb("neg_ident", [P, P], F16)
        pick = sb("pick", [P, N], F32R)
        ones = sb("ones", [P, 1])
        minus_half, eps = sb("minus_half", [P, TJ]), sb("eps", [P, TJ])
        a_coef = sb("a_coef", [P, EH, N])
        inv_a = sb("inv_a", [P, EH, N])
        inv_a_t = sb("inv_a_t", [P, E])
        tiny = sb("tiny", [P, EH, N])
        kept = sb("kept", [P, EH, N])
        d_skip = sb("d_skip", [P, EH])
        flag = sb("flag", [1, 1], I32)
        flag_f = sb("flag_f", [1, 1])

        inv_a_u = hid[:, 0, 0:EH * PROWS].rearrange("p (h n) -> p h n", h=EH)
        flat = ring[:].rearrange("p s n -> p (s n)")
        st_g = flat[:, 0:HM * E]
        st_u = flat[:, HM * E:2 * HM * E]
        st_d = flat[:, 2 * HM * E:3 * HM * E]
        o = 3 * HM * E
        st_z, st_o = flat[:, o:o + EH * E], flat[:, o + EH * E:o + 2 * EH * E]
        o += 2 * EH * E
        st_p, st_dt = flat[:, o:o + E], flat[:, o + E:o + E + EH * R]

        work = [ctx.enter_context(nc.psum_tensor(f"work{i}", [P, CH], F32)) for i in range(BANKS)]
        c_bank = ctx.enter_context(nc.psum_tensor("c_bank", [P, L], F32))

        ready = [sem(f"bank_ready{i}") for i in range(BANKS)]
        free = [sem(f"bank_free{i}") for i in range(BANKS)]
        S = {s: sem(s) for s in K.slope}
        w_landed, w_set, w_turned, w_kept = sem("w_landed"), sem("w_set"), sem("w_turned"), sem("w_kept")
        s_ident, s_exp, s_set, s_flag, s_fix = sem("s_ident"), sem("s_exp"), sem("s_set"), sem("s_flag"), sem("s_fix")

        def wait(eng, what, step, turn, less=0, apart=False):
            if (what, step) not in K.at:
                return
            s, n = K.at[what, step]
            n -= less
            if what in ("ready", "free"):
                s, slope = (ready if what == "ready" else free)[s], K.bank_slope
            else:
                s, slope = S[s], K.slope[s]
            if turn is not None:
                n = eng.to_reg(turn * slope + n) if apart else turn * slope + n
                if apart:
                    eng.wait_ge(s_set, 1)
            eng.wait_ge(s, n)

        def wait_before(eng, what, step, back, turn):
            before = K.prev[what, step]
            if len(before) >= back:
                wait(eng, what, before[-back], turn)

        def bank(job):
            return work[K.bank[job]]

        def done(job):
            return ready[K.bank[job]]

        def freed(job):
            return free[K.bank[job]]

        def parts(eng, part):
            for b in range(-1, LOOP_FROM):
                part(b, None)
            with eng.Fori(0, (LOOP_TO - LOOP_FROM) // 2) as turn:
                for b in (LOOP_FROM, LOOP_FROM + 1):
                    part(b, turn)
            for b in range(LOOP_TO, B + 1):
                part(b, None)

        def row(b, turn):
            return b if turn is None else turn * 2 + b

        groups = 8 + 3 + 1 + 1 + 1 + 1 + 1

        block = ctx.enter_context(nc.Block())

        @block.sync
        def _(sp):
            for dst, src in (
                (st_g.bitcast(I32).rearrange("p (m e) -> p m e", m=HM), w_gate.rearrange("(m p) e -> p m e", p=P)),
                (st_u.bitcast(I32).rearrange("p (m e) -> p m e", m=HM), w_up.rearrange("(m p) e -> p m e", p=P)),
                (st_d.bitcast(I32).rearrange("p (h k) -> p h k", h=EH), w_down.rearrange("(h p) k -> p h k", p=P)),
                (st_z.rearrange("p (h e) -> p h e", h=EH), W_z.rearrange("(h p) e -> p h e", p=P)),
                (st_o.rearrange("p (h e) -> p h e", h=EH), W_out.rearrange("(h p) e -> p h e", p=P)),
                (st_p[0:R + 2 * N, :], W_params),
                (st_dt.rearrange("p (h r) -> p h r", h=EH), W_dt.rearrange("(h p) r -> p h r", p=P)),
                (a_coef[:], A_log.rearrange("(h p) n -> p h n", p=P)),
                (taps[:], conv_w.rearrange("(h p) o k -> p h (o k)", p=P)),
                (wdt_t[R:R + 1, :], b_dt.rearrange("(o e) -> o e", o=1)),
            ):
                sp.dma_start(dst, src).then_inc(w_landed, 16)
            with nc.allow_non_contiguous_dma(reason="256 numbers, one to a partition"):
                sp.dma_start(d_skip[:], D.rearrange("(h p) -> p h", p=P)).then_inc(w_landed, 16)

            def part(b, turn):
                for ev in steps(b):
                    if ev[0] == "ld":
                        _, bt, c = ev
                        wait(sp, "free", ("dn", 1, bt - 1, c, 1), turn)
                        src = x[row(bt, turn)].rearrange("(c j p) e -> c p j e", c=NC, p=P)[c]
                        sp.dma_start(x_in[:, c * TJ:(c + 1) * TJ, :], src).then_inc(S[f"ld{c}"], 16)
                    elif ev[0] == "st":
                        _, bt, c = ev
                        wait(sp, "free", ("dn", 2, bt, c, 1), turn)
                        dst = out[row(bt, turn)].rearrange("(c j p) e -> c p j e", c=NC, p=P)[c]
                        sp.dma_start(dst, x_fin[:, c * TJ:(c + 1) * TJ, :]).then_inc(S[f"st{c}"], 16)

            parts(sp, part)
            for c in range(NC):
                sp.wait_ge(S[f"st{c}"], 16 * B)

        @block.tensor
        def _(pe):
            pe.wait_ge(s_ident, 2)
            pe.wait_ge(w_set, 3)
            n = 0

            def turn_group(blocks):
                nonlocal n
                if n >= BANKS:
                    pe.wait_ge(w_kept, n - BANKS + 1)
                for i, src in enumerate(blocks):
                    k, m = src.shape
                    last = pe.transpose(work[n % BANKS][0:m, i * P:i * P + k], src, ident[0:k, 0:k])
                last.then_inc(w_turned, 1)
                n += 1

            for w in (st_g, st_u):
                for k in range(EH):
                    for m0 in (0, 4):
                        turn_group([w[:, m * E + k * P:m * E + (k + 1) * P] for m in range(m0, min(m0 + 4, HM))])
            for m0 in range(0, HM, 2):
                turn_group([st_d[:, h * HID + m * P:h * HID + (m + 1) * P] for m in (m0, m0 + 1) for h in range(EH)])
            for w in (st_z, st_o):
                turn_group([w[:, h * E + k * P:h * E + (k + 1) * P] for k in range(EH) for h in range(EH)])
            turn_group([st_p[0:R + 2 * N, k * P:(k + 1) * P] for k in range(EH)])
            turn_group([st_dt[:, h * R:(h + 1) * R] for h in range(EH)])
            pe.wait_ge(s_set, 1)
            turn_group([inv_a_u[:, h, :] for h in range(EH)])
            pe.matmul(c_bank[0:1, 0:EH * N], ones[:], tiny[:].rearrange("p h n -> p (h n)"), start=True,
                      stop=True).then_inc(s_flag, 1)
            pe.wait_ge(w_kept, groups)
            pe.wait_ge(s_flag, 4)

            def part(b, turn):
                def take(job):
                    s, n = K.at["free", job]
                    if n > 1:
                        n -= 1
                        pe.wait_ge(free[s], n if turn is None else turn * K.bank_slope + n)
                    return bank(job)

                for ev in steps(b):
                    kind = ev[0]
                    if kind == "T":
                        wait(pe, "normed", ("lx",) + ev[1:], turn)
                        for h in range(EH):
                            job = ev + (h,)
                            dst = take(job)
                            for j in range(TJ):
                                block = normed[:, j, h * P:(h + 1) * P]
                                if ev[1] == 2:
                                    last = pe.transpose(dst[:, j * P:(j + 1) * P], block, ident[:])
                                else:
                                    last = pe.matmul(dst[:, j * P:(j + 1) * P], block, ident[:], start=(j == 0),
                                                     stop=(j == TJ - 1))
                            last.then_inc(done(job), 1)
                    elif kind == "Ts":
                        _, f, bt, c = ev
                        for h in range(EH):
                            wait(pe, "xhi", ("Te",) + ev[1:], turn, less=EH - 1 - h)
                            pe.matmul(bank(("T",) + ev[1:] + (h,))[:], neg_ident[:], xt_hi[c][:, h, :], start=False,
                                      stop=True, skip_group_check=True).then_inc(S["lowered"], 1)
                    elif kind == "gu":
                        _, f, bt, c, m = ev
                        wait(pe, "free", ("T", 1 if f == 1 else 3, bt, c, EH - 1), turn)
                        for w, name in ((wg_t, "gate"), (wu_t, "up")):
                            job = ev + (name,)
                            dst = take(job)
                            for k in range(EH):
                                for i, part_ in enumerate((xt_hi[c], xt_lo[c])):
                                    last = pe.matmul(dst[:], w[:, k, m * P:(m + 1) * P], part_[:, k, :],
                                                     start=(k == 0 and i == 0), stop=(k == EH - 1 and i == 1))
                            last.then_inc(done(job), 1)
                    elif kind == "dn":
                        _, f, bt, c, jp = ev
                        wait(pe, "lo", ("lo", f, bt, c, HM - 1), turn)
                        dst = take(ev)
                        for j in range(2):
                            t = (2 * jp + j) * P
                            for m in range(HM):
                                for i, part_ in enumerate((hid_hi, hid_lo)):
                                    last = pe.matmul(dst[:, j * E:(j + 1) * E], part_[:, m, t:t + P], wd_t[:, m, :],
                                                     start=(m == 0 and i == 0), stop=(m == HM - 1 and i == 1))
                        last.then_inc(done(ev), 1)
                    elif kind == "op":
                        _, bt, jp = ev
                        wait(pe, "gated", ("gate", bt), turn)
                        dst = take(ev)
                        for j in range(2):
                            t = (2 * jp + j) * P
                            for h in range(EH):
                                last = pe.matmul(dst[:, j * E:(j + 1) * E], acc[bt % 2][:, h, t:t + P], wo_t[:, h, :],
                                                 start=(h == 0), stop=(h == EH - 1))
                        last.then_inc(done(ev), 1)
                    elif kind == "z":
                        _, bt, h, c = ev
                        dst = take(ev)
                        for k in range(EH):
                            last = pe.matmul(dst[:], wz_t[:, k, h * P:(h + 1) * P],
                                             xt[:, k, KW - 1 + c * CH:KW - 1 + (c + 1) * CH],
                                             start=(k == 0), stop=(k == EH - 1))
                        last.then_inc(done(ev), 1)
                    elif kind == "pm":
                        _, bt, c = ev
                        wait(pe, "free", ("T", 2, bt, c, EH - 2), turn)
                        wait(pe, "free", ("T", 2, bt, c, EH - 1), turn)
                        dst = take(ev)
                        for k in range(EH):
                            last = pe.matmul(dst[0:PROWS, :], wp_t[:, k, :],
                                             xt[:, k, KW - 1 + c * CH:KW - 1 + (c + 1) * CH],
                                             start=(k == 0), stop=(k == EH - 1))
                        last.then_inc(done(ev), 1)
                    elif kind == "cv":
                        _, bt, h, c = ev
                        dst = take(ev)
                        for k in range(KW):
                            last = pe.matmul(dst[:], tap_diag[:, h, k, :], xt[:, h, k + c * CH:k + (c + 1) * CH],
                                             start=(k == 0), stop=(k == KW - 1))
                        last.then_inc(done(ev), 1)
                    elif kind == "dt":
                        _, bt, h, c = ev
                        wait(pe, "c_high", ("pe", bt, c), turn)
                        dst = take(ev)
                        pe.matmul(dst[:], wdt_t[:, h * P:(h + 1) * P], params[0:R + 1, c * CH:(c + 1) * CH],
                                  start=True, stop=True).then_inc(done(ev), 1)
                    elif kind == "rm":
                        _, bt, h, c = ev
                        wait(pe, "c_high", ("pe", bt, c), turn)
                        dst = take(ev)
                        pe.matmul(dst[:], inv_a_t[CD_ROW:CD_ROW + N, h * P:(h + 1) * P],
                                  params[CD_ROW:CD_ROW + N, c * CH:(c + 1) * CH],
                                  start=True, stop=True).then_inc(done(ev), 1)
                    elif kind == "bc":
                        _, bt, s = ev
                        wait(pe, "free", ("pm", bt, NC - 1), turn)
                        if s:
                            wait(pe, "weighted", ("cm", bt, s - 1, EH - 1), turn)
                        else:
                            wait(pe, "weighted", ("cm", bt - 1, N - 1, EH - 1), turn)
                        for c in range(NC):
                            last = pe.matmul(c_bank[:, c * CH:(c + 1) * CH], pick[C_ROW:P, s:s + 1].to_broadcast([P - C_ROW, P]),
                                             c_parts[bt % 2][C_ROW:P, c * CH:(c + 1) * CH], start=True, stop=True)
                        last.then_inc(S["c_spread"], 1)

            parts(pe, part)

        @block.scalar
        def _(act):
            act.wait_ge(w_landed, 16 * 11)
            nc.scalar.activation(a_coef[:], a_coef[:], ACT.Exp).then_inc(s_exp, 1)
            act.wait_ge(w_kept, groups)
            act.wait_ge(s_set, 1)

            def part(b, turn):
                for ev in steps(b):
                    kind = ev[0]
                    if kind == "lx":
                        _, f, bt, c = ev
                        slot = K.at["normed", ev][1] % 2
                        src = {1: x_in, 2: x_mid[bt % 2], 3: x_fin}[f]
                        wait(act, "ready", K.was[ev], turn)
                        wait(act, "rstd", ("lr",) + ev[1:], turn)
                        for j in range(TJ):
                            last = nc.scalar.activation(normed[:, j, :], src[:, c * TJ + j, :], ACT.Identity,
                                                        bias=shift[:, slot, j:j + 1], scale=rstd[:, slot, j:j + 1])
                        last.then_inc(S["normed"], 1)
                    elif kind == "Te":
                        _, f, bt, c = ev
                        for h in range(EH):
                            job = ("T", f, bt, c, h)
                            wait(act, "ready", job, turn)
                            if f == 2:
                                if h == 0:
                                    wait(act, "ready", ("z", bt - 1, EH - 1, NC - 1), turn)
                                nc.scalar.activation(xt[:, h, KW - 1 + c * CH:KW - 1 + (c + 1) * CH], bank(job)[:],
                                                     ACT.Copy).then_inc(freed(job), 1)
                            else:
                                if h == 0:
                                    wait(act, "ready", K.was["T", f, bt, c], turn)
                                nc.scalar.activation(xt_hi[c][:, h, :], bank(job)[:], ACT.Copy, scale=XS).then_inc(S["xhi"], 1)
                    elif kind == "Tl":
                        _, f, bt, c = ev
                        for h in range(EH):
                            wait(act, "lowered", ("Ts",) + ev[1:], turn, less=EH - 1 - h)
                            job = ("T",) + ev[1:] + (h,)
                            nc.scalar.activation(xt_lo[c][:, h, :], bank(job)[:], ACT.Copy, scale=XS).then_inc(freed(job), 1)
                    elif kind == "th":
                        job = ev[1:] + (("gate",) if ev[1] == "gu" else ())
                        wait(act, "ready", job, turn)
                        before = K.prev["tanh", ev]
                        if len(before) == TANHS:
                            was = before[0][1:]
                            wait(act, "free", was + ("gate",) if was[0] == "gu" else was, turn)
                        slot = K.at["tanh", ev][1] % TANHS
                        nc.scalar.activation(tanh[:, slot, :], bank(job)[:], ACT.Tanh,
                                             scale=GATE_HALF if ev[1] == "gu" else 0.5).then_inc(S["tanh"], 1)
                    elif kind == "hi":
                        _, f, bt, c, m = ev
                        wait(act, "free", ("gu",) + ev[1:] + ("up",), turn)
                        if m == 0:
                            wait(act, "ready", K.was[ev], turn)
                        slot = K.at["hi", ev][1] % HIDS
                        nc.scalar.activation(hid_hi[:, m, :], hid[:, slot, :], ACT.Copy).then_inc(S["hi"], 1)
                    elif kind == "pe":
                        _, bt, c = ev
                        job = ("pm", bt, c)
                        wait(act, "ready", job, turn)
                        wait(act, "ready", ("rm", bt - 1, EH - 1, c), turn)
                        wait(act, "c_spread", ("bc", bt - 2, N - 1), turn)
                        src, t = bank(job), slice(c * CH, (c + 1) * CH)
                        nc.scalar.activation(params[0:R, t], src[0:R, :], ACT.Copy)
                        nc.scalar.activation(params[CD_ROW:CD_ROW + N, t], src[CD_ROW:CD_ROW + N, :], ACT.Copy)
                        nc.scalar.activation(c_parts[bt % 2][C_ROW:C_ROW + N, t], src[C_ROW:C_ROW + N, :], ACT.Copy)
                        nc.scalar.activation(c_parts[bt % 2][CD_ROW:CD_ROW + N, t], src[CD_ROW:CD_ROW + N, :],
                                             ACT.Copy).then_inc(S["c_high"], 1)
                    elif kind == "da":
                        _, bt, h, c = ev
                        job = ("dt",) + ev[1:]
                        wait(act, "ready", job, turn)
                        wait(act, "scanned", ("scan", bt - 2, N - 1, EH - 1), turn)
                        y = dt[bt % 2][:, h, 1 + c * CH:1 + (c + 1) * CH]
                        nc.scalar.activation(y, bank(job)[:], ACT.Abs).then_inc(S["sp_exp"], 1)
                        wait(act, "sp_sum", ("dp", bt, h - 1, c) if h else ("dp", bt - 1, EH - 1, c), turn)
                        nc.scalar.activation(sp_r[:, c, :], bank(job)[:], ACT.Relu).then_inc(freed(job), 1)
                        wait(act, "sp_exp", ev, turn, less=1)
                        nc.scalar.activation(y, y, ACT.Exp, scale=-1.0).then_inc(S["sp_exp"], 1)
                    elif kind == "dl":
                        _, bt, h, c = ev
                        wait(act, "sp_exp", ("da", bt, h, c), turn)
                        wait(act, "sp_sum", ("dp", bt, h - 1, c) if h else ("dp", bt - 1, EH - 1, c), turn)
                        nc.scalar.activation(sp_l[:, c, :], dt[bt % 2][:, h, 1 + c * CH:1 + (c + 1) * CH], ACT.Copy,
                                             bias=1.0).then_inc(S["sp_ln"], 1)
                        wait(act, "sp_ln", ev, turn, less=2)
                        nc.scalar.activation(sp_v[:, c, :], sp_l[:, c, :], ACT.Copy, bias=-1.0).then_inc(S["sp_ln"], 1)
                        wait(act, "sp_ln", ev, turn, less=1)
                        nc.scalar.activation(sp_l[:, c, :], sp_l[:, c, :], ACT.Ln).then_inc(S["sp_ln"], 1)
                    elif kind == "ex":
                        _, bt, s, h = ev
                        if s == 0 and h == 0:
                            wait(act, "dt_first", ("dt0", bt), turn)
                        before = K.prev["decay", ev]
                        if len(before) >= DECAYS:
                            wait(act, "scanned", ("scan",) + before[-DECAYS][1:], turn)
                        slot = K.at["decay", ev][1] % DECAYS
                        nc.scalar.activation(decay[:, slot, :], dt[bt % 2][:, h, 0:L], ACT.Exp,
                                             scale=a_coef[:, h, s:s + 1]).then_inc(S["decay"], 1)

            parts(act, part)

        @block.gpsimd
        def _(pool):
            nc.gpsimd.memset(ident[:], 0.0).then_inc(s_ident, 1)
            pool.wait_ge(s_ident, 1)
            nc.gpsimd.affine_select(out=ident[:], in_=ident[:], compare_op=ALU.not_equal, fill=1.0, base=0,
                                    pattern=[[-1, P]], channel_multiplier=1).then_inc(s_ident, 1)
            pool.wait_ge(w_kept, groups)
            pool.wait_ge(s_set, 1)
            def part(b, turn):
                for ev in steps(b):
                    kind = ev[0]
                    if kind == "lr":
                        _, f, bt, c = ev
                        slot = K.at["rstd", ev][1] // 4 % 2
                        r = rstd[:, slot, :]
                        before = K.prev["rstd", ev]
                        if len(before) >= 2:
                            wait(pool, "normed", ("lx",) + before[-2][1:], turn)
                        wait(pool, "meanvar", ("ln",) + ev[1:], turn)
                        nc.gpsimd.tensor_tensor(r, meanvar[:, slot, :, 1], eps[:], ALU.add).then_inc(S["rstd"], 1)
                        wait(pool, "rstd", ev, turn, less=3)
                        nc.gpsimd.tensor_tensor(r, r, minus_half[:], ALU.pow).then_inc(S["rstd"], 1)
                        wait(pool, "rstd", ev, turn, less=2)
                        nc.gpsimd.tensor_tensor(shift[:, slot, :], meanvar[:, slot, :, 0], r, ALU.mult).then_inc(S["rstd"], 1)
                        wait(pool, "rstd", ev, turn, less=1, apart=True)
                        nc.gpsimd.tensor_scalar(shift[:, slot, :], shift[:, slot, :], -1.0, None, ALU.mult).then_inc(S["rstd"], 1)
                    elif kind == "lo":
                        m = ev[4]
                        wait(pool, "hi", ("hi",) + ev[1:], turn)
                        slot = K.at["lo", ev][1] % HIDS
                        nc.gpsimd.tensor_tensor(hid_lo[:, m, :], hid[:, slot, :], hid_hi[:, m, :],
                                                ALU.subtract).then_inc(S["lo"], 1)
                    elif kind == "dp":
                        _, bt, h, c = ev
                        y = dt[bt % 2][:, h, 1 + c * CH:1 + (c + 1) * CH]
                        wait(pool, "sp_ln", ("dl", bt, h, c), turn)
                        nc.gpsimd.tensor_tensor(sp_l[:, c, :], sp_l[:, c, :], sp_v[:, c, :],
                                                ALU.subtract).then_inc(S["sp_sum"], 1)
                        wait(pool, "sp_sum", ev, turn, less=2)
                        nc.gpsimd.tensor_tensor(y, sp_l[:, c, :], y, ALU.add).then_inc(S["sp_sum"], 1)
                        wait(pool, "sp_sum", ev, turn, less=1)
                        nc.gpsimd.tensor_tensor(y, sp_r[:, c, :], y, ALU.add).then_inc(S["sp_sum"], 1)
                    elif kind == "gate":
                        _, bt = ev
                        for h in range(EH):
                            wait(pool, "summed", ("cm", bt, N - 1, h), turn)
                            if h == 0:
                                wait(pool, "free", ("z", bt, EH - 1, NC - 1), turn)
                            nc.gpsimd.tensor_tensor(acc[bt % 2][:, h, :], acc[bt % 2][:, h, :], zs[:, h, :],
                                                    ALU.mult).then_inc(S["gated"], 1)
                    elif kind == "cm":
                        _, bt, s, h = ev
                        if s == 0 and h == 0:
                            wait(pool, "acc_begun", ("ai", bt, EH - 1, NC - 1), turn)
                        wait(pool, "weighted", ev, turn)
                        wait_before(pool, "summed", ev, 2, turn)
                        slot = K.at["weighted", ev][1] % TERMS
                        nc.gpsimd.tensor_tensor(acc[bt % 2][:, h, :], acc[bt % 2][:, h, :], cg[:, slot, :],
                                                ALU.add).then_inc(S["summed"], 1)
                    elif kind == "d":
                        _, bt, h = ev
                        if h == 0:
                            wait(pool, "u_first", ("u0", bt), turn)
                        wait(pool, "scanned", ("scan", bt - 1, N - 1, h), turn)
                        nc.gpsimd.tensor_tensor(du[:, h, :], u[bt % 2][:, h, 1:1 + L], u[bt % 2][:, h, 0:L],
                                                ALU.subtract).then_inc(S["du"], 1)

            parts(pool, part)

        @block.vector
        def _(dve):
            own = 0

            def then(ins):
                nonlocal own
                own += 1
                ins.then_inc(w_set, 1)
                dve.wait_ge(w_set, own)

            dve.wait_ge(w_landed, 16 * 11)
            for w in (st_g, st_u, st_d):
                then(nc.vector.tensor_copy(w, w.bitcast(I32)))
            for t in (wp_t[:], inv_a_u, pick[:].bitcast(F32), c_parts[0][:].bitcast(F32), c_parts[1][:].bitcast(F32),
                      xt[:, :, 0:KW - 1], u[0][:, :, 0:1], u[1][:, :, 0:1], params[C_ROW:P, :]):
                then(nc.vector.memset(t, 0.0))
            then(nc.vector.memset(ones[:], 1.0))
            then(nc.vector.memset(minus_half[:], -0.5))
            then(nc.vector.memset(eps[:], EPS))
            then(nc.vector.memset(params[R:R + 1, :], 1.0))
            dve.wait_ge(s_ident, 2)
            then(nc.vector.tensor_scalar(neg_ident[:], ident[:], -1.0 / XS, None, ALU.mult))
            then(nc.vector.tensor_copy(pick[C_ROW:C_ROW + N, :], ident[C_ROW:C_ROW + N, C_ROW:C_ROW + N]))
            then(nc.vector.tensor_copy(pick[CD_ROW:CD_ROW + N, :], ident[CD_ROW:CD_ROW + N, CD_ROW:CD_ROW + N]))
            for h in range(EH):
                for k in range(KW):
                    then(nc.vector.tensor_scalar(tap_diag[:, h, k, :], ident[:], taps[:, h, k:k + 1], None, ALU.mult))
            dve.wait_ge(s_exp, 1)
            then(nc.vector.tensor_scalar(tiny[:], a_coef[:], A_MIN, None, ALU.is_lt))
            then(nc.vector.tensor_scalar(a_coef[:], a_coef[:], -1.0, None, ALU.mult))
            then(nc.vector.tensor_scalar(kept[:], tiny[:], -1.0, 1.0, ALU.mult, ALU.add))
            then(nc.vector.scalar_tensor_tensor(inv_a[:], a_coef[:], 1e-10, kept[:], ALU.add, ALU.mult))
            then(nc.vector.tensor_tensor(inv_a[:], inv_a[:], tiny[:], ALU.subtract))
            then(nc.vector.reciprocal(inv_a[:], inv_a[:]))
            then(nc.vector.tensor_tensor(inv_a[:], inv_a[:], kept[:], ALU.mult))
            then(nc.vector.tensor_copy(inv_a_u[:, :, CD_ROW:CD_ROW + N], inv_a[:]))
            then(nc.vector.tensor_tensor(inv_a[:], inv_a[:], tiny[:], ALU.add))
            nc.vector.tensor_copy(flag_f[:], ones[0:1, :]).then_inc(s_set, 1)
            n = 0

            def keep(copies):
                nonlocal n
                dve.wait_ge(w_turned, n + 1)
                for dst, src in copies(work[n % BANKS]):
                    last = nc.vector.tensor_copy(dst, src)
                last.then_inc(w_kept, 1)
                n += 1

            for w in (wg_t, wu_t):
                for k in range(EH):
                    for m0, m1 in ((0, 4), (4, HM)):
                        keep(lambda ps: [(w[:, k, m0 * P:m1 * P], ps[:, 0:(m1 - m0) * P])])
            for m0 in range(0, HM, 2):
                keep(lambda ps: [(wd_t[:, m0:m0 + 2, :].rearrange("p m e -> p (m e)"), ps[:])])
            for w in (wz_t, wo_t):
                keep(lambda ps: [(w[:].rearrange("p k e -> p (k e)"), ps[:])])
            dve.wait_ge(w_kept, n)
            nc.vector.tensor_scalar(wo_t[:], wo_t[:], 0.25, None, ALU.mult).then_inc(s_flag, 1)
            keep(lambda ps: [(wp_t[:, k, a:a + m], ps[:, k * P + o:k * P + o + m]) for k in range(EH)
                             for a, o, m in ((0, 0, R), (C_ROW, R + N, N), (CD_ROW, R + N, N))])
            keep(lambda ps: [(wdt_t[0:R, :], ps[0:R, 0:E])])
            keep(lambda ps: [(inv_a_t[CD_ROW:CD_ROW + N, :], ps[CD_ROW:CD_ROW + N, 0:E])])
            dve.wait_ge(s_flag, 2)
            nc.vector.tensor_reduce(flag_f[:], c_bank[0:1, 0:EH * N], AX_X, ALU.add).then_inc(s_flag, 1)
            dve.wait_ge(s_flag, 3)
            nc.vector.tensor_copy(flag[:], flag_f[:]).then_inc(s_flag, 1)
            dve.wait_ge(s_flag, 4)
            dve.wait_ge(w_kept, groups)
            n_tiny = dve.value_load(flag[0:1, 0:1])

            def program(with_tiny):
                def part(b, turn):
                    for ev in steps(b):
                        kind = ev[0]
                        if kind == "ln":
                            _, f, bt, c = ev
                            slot = K.at["meanvar", ev][1] % 2
                            src = {1: x_in, 2: x_mid[bt % 2], 3: x_fin}[f]
                            if f == 1:
                                wait(dve, f"ld{c}", ("ld", bt, c), turn)
                            elif f == 2:
                                wait(dve, "free", ("dn", 1, bt, c, 1), turn)
                            else:
                                wait(dve, "free", ("op", bt, 2 * c + 1), turn)
                            before = K.prev["meanvar", ev]
                            if len(before) >= 2:
                                wait(dve, "normed", ("lx",) + before[-2][1:], turn)
                            for j in range(TJ):
                                last = nc.vector.bn_stats(stats[:, slot, j, :], src[:, c * TJ + j, :])
                            last.then_inc(S["stats"], 1)
                            wait(dve, "stats", ev, turn, apart=True)
                            for j in range(TJ):
                                last = nc.vector.bn_aggr(meanvar[:, slot, j, :], stats[:, slot, j, :])
                            last.then_inc(S["meanvar"], 1)
                        elif kind == "sh":
                            gu = ("gu",) + ev[1:]
                            wait(dve, "tanh", ("th",) + gu, turn)
                            i = K.at["lo", ("lo",) + ev[1:]][1] % HIDS
                            wait_before(dve, "lo", ("lo",) + ev[1:], HIDS, turn)
                            nc.vector.scalar_tensor_tensor(hid[:, i, :], tanh[:, K.at["tanh", ("th",) + gu][1] % TANHS, :], 1.0,
                                                           bank(gu + ("gate",))[:], ALU.add,
                                                           ALU.mult).then_inc(freed(gu + ("gate",)), 1)
                            wait(dve, "free", gu + ("gate",), turn)
                            wait(dve, "ready", gu + ("up",), turn)
                            nc.vector.scalar_tensor_tensor(hid[:, i, :], hid[:, i, :], H_SCALE, bank(gu + ("up",))[:],
                                                           ALU.mult, ALU.mult).then_inc(freed(gu + ("up",)), 1)
                        elif kind == "rs":
                            _, f, bt, c, jp = ev
                            job = ("dn",) + ev[1:]
                            t = slice(c * TJ + 2 * jp, c * TJ + 2 * jp + 2)
                            src, dst = (x_in, x_mid[bt % 2]) if f == 1 else (x_fin, x_fin)
                            wait(dve, "ready", job, turn)
                            nc.vector.scalar_tensor_tensor(
                                dst[:, t, :].rearrange("p j e -> p (j e)"), bank(job)[:], OUT_SCALE,
                                src[:, t, :].rearrange("p j e -> p (j e)"), ALU.mult, ALU.add).then_inc(freed(job), 1)
                        elif kind == "ra":
                            _, bt, jp = ev
                            job = ("op", bt, jp)
                            t = slice(2 * jp, 2 * jp + 2)
                            wait(dve, f"st{jp // 2}", ("st", bt - 1, jp // 2), turn)
                            wait(dve, "ready", job, turn)
                            nc.vector.tensor_tensor(
                                x_fin[:, t, :].rearrange("p j e -> p (j e)"), bank(job)[:],
                                x_mid[bt % 2][:, t, :].rearrange("p j e -> p (j e)"), ALU.add).then_inc(freed(job), 1)
                        elif kind == "zs":
                            _, bt, h, c = ev
                            job = ("z",) + ev[1:]
                            wait(dve, "tanh", ("th",) + job, turn)
                            wait(dve, "gated", ("gate", bt - 1), turn)
                            nc.vector.scalar_tensor_tensor(zs[:, h, c * CH:(c + 1) * CH], tanh[:, K.at["tanh", ("th",) + job][1] % TANHS, :], 1.0,
                                                           bank(job)[:], ALU.add, ALU.mult).then_inc(freed(job), 1)
                        elif kind == "pl":
                            _, bt = ev
                            for c in range(NC):
                                job = ("pm", bt, c)
                                wait(dve, "c_high", ("pe", bt, c), turn)
                                low = c_parts[bt % 2][CD_ROW:CD_ROW + N, c * CH:(c + 1) * CH]
                                nc.vector.tensor_tensor(low, bank(job)[CD_ROW:CD_ROW + N, :], low.bitcast(F32),
                                                        ALU.subtract).then_inc(freed(job), 1)
                        elif kind == "us":
                            _, bt, h, c = ev
                            job = ("cv",) + ev[1:]
                            wait(dve, "tanh", ("th",) + job, turn)
                            wait(dve, "du", ("d", bt - 2, EH - 1), turn)
                            nc.vector.scalar_tensor_tensor(u[bt % 2][:, h, 2 + c * CH:2 + (c + 1) * CH],
                                                           tanh[:, K.at["tanh", ("th",) + job][1] % TANHS, :], 1.0, bank(job)[:],
                                                           ALU.add, ALU.mult).then_inc(freed(job), 1)
                        elif kind == "u0":
                            _, bt = ev
                            wait(dve, "free", ("cv", bt, EH - 1, 0), turn)
                            nc.vector.tensor_copy(u[bt % 2][:, :, 1:2], u[bt % 2][:, :, 2:3]).then_inc(S["u_first"], 1)
                        elif kind == "dt0":
                            _, bt = ev
                            wait(dve, "sp_sum", ("dp", bt, EH - 1, NC - 1), turn)
                            nc.vector.tensor_copy(dt[bt % 2][:, :, 0:1], dt[bt % 2][:, :, 1:2]).then_inc(S["dt_first"], 1)
                        elif kind == "ai":
                            _, bt, h, c = ev
                            job = ("rm",) + ev[1:]
                            t = acc[bt % 2][:, h, c * CH:(c + 1) * CH]
                            wait(dve, "ready", job, turn)
                            wait(dve, "u_first", ("u0", bt), turn)
                            nc.vector.tensor_tensor(t, bank(job)[:], u[bt % 2][:, h, 1 + c * CH:1 + (c + 1) * CH],
                                                    ALU.mult).then_inc(freed(job), 1)
                            wait(dve, "free", job, turn)
                            nc.vector.scalar_tensor_tensor(t, u[bt % 2][:, h, 2 + c * CH:2 + (c + 1) * CH], d_skip[:, h:h + 1], t,
                                                           ALU.mult, ALU.subtract).then_inc(S["acc_begun"], 1)
                        elif kind == "scan":
                            _, bt, s, h = ev
                            i, a = K.at["scanned", ev][1] % 2, K.at["decay", ("ex",) + ev[1:]][1] % DECAYS
                            if s == 0:
                                wait(dve, "du", ("d", bt, h), turn)
                            wait(dve, "decay", ("ex",) + ev[1:], turn)
                            was = K.prev["scanned", ev][-2:]
                            if len(was) == 2:
                                wait(dve, "weighted", ("cm",) + was[0][1:], turn)
                            scan = nc.vector.tensor_tensor_scan(g[:, i, :], du[:, h, :], decay[:, a, :], 0.0, ALU.add, ALU.mult)
                            if not with_tiny:
                                scan.then_inc(S["scanned"], 1)
                                continue
                            _, k = K.at["scanned", ev]
                            at = 4 * (k - 1) if turn is None else turn * (4 * K.slope["scanned"]) + 4 * (k - 1)
                            scan.then_inc(s_fix, 1)
                            before = K.prev["weighted", ("cm",) + ev[1:]][-TERMS:]
                            if len(before) == TERMS:
                                wait(dve, "summed", before[0], turn)
                            v = cg[:, K.at["weighted", ("cm",) + ev[1:]][1] % TERMS, :]
                            nc.vector.scalar_tensor_tensor(v, dt[bt % 2][:, h, 0:L], tiny[:, h, s:s + 1], u[bt % 2][:, h, 1:1 + L],
                                                           ALU.mult, ALU.mult).then_inc(s_fix, 1)
                            dve.wait_ge(s_fix, at + 2)
                            nc.vector.tensor_tensor_scan(v, decay[:, a, :], v, 0.0, ALU.mult, ALU.add).then_inc(s_fix, 1)
                            dve.wait_ge(s_fix, at + 3)
                            nc.vector.tensor_scalar(g[:, i, :], g[:, i, :], kept[:, h, s:s + 1], None, ALU.mult).then_inc(s_fix, 1)
                            dve.wait_ge(s_fix, at + 4)
                            nc.vector.tensor_tensor(g[:, i, :], g[:, i, :], v, ALU.add).then_inc(S["scanned"], 1)
                        elif kind == "cm":
                            _, bt, s, h = ev
                            i, k = K.at["weighted", ev][1] % 2, K.at["weighted", ev][1] % TERMS
                            wait(dve, "scanned", ("scan",) + ev[1:], turn)
                            wait(dve, "c_spread", ("bc", bt, s), turn)
                            was = K.prev["weighted", ev][-TERMS:]
                            if len(was) == TERMS:
                                wait(dve, "summed", was[0], turn)
                            nc.vector.scalar_tensor_tensor(cg[:, k, :], g[:, i, :], inv_a[:, h, s:s + 1], c_bank[:],
                                                           ALU.mult, ALU.mult).then_inc(S["weighted"], 1)

                parts(dve, part)

            with dve.If(n_tiny > 0):
                program(True)
            with dve.Else():
                program(False)


INS = ("L0_attn_x", "L0_attn_W_z", "L0_attn_W_params", "L0_attn_conv_w", "L0_attn_W_dt", "L0_attn_b_dt", "L0_attn_A_log",
       "L0_attn_D", "L0_attn_W_out", "L0_ffn_w_gate", "L0_ffn_w_up", "L0_ffn_w_down")


def kernel(**inputs):
    import concourse.bacc as bacc
    from concourse.bass_utils import run_bass_kernel_spmd

    nc = bacc.Bacc("TRN2", target_bir_lowering=False, num_devices=1, dynamic_dma_scratch_size=1024)
    arrays, args = {}, []
    for name in INS:
        a = np.ascontiguousarray(inputs[name])
        arrays[name] = a
        args.append(nc.dram_tensor(name, a.shape, mybir.dt.from_np(a.dtype), kind="ExternalInput").ap())
    out = nc.dram_tensor("out", (B, L, E), F32, kind="ExternalOutput").ap()
    macaron_kernel(nc, *args, out)
    return run_bass_kernel_spmd(nc, [arrays], core_ids=[0]).results[0]["out"]
```
